# Optimizing a Trainium2 kernel written in Bass

```python
import numpy as np
import jax
import jax.numpy as jnp

def _softmax(x, axis=-1):
    return jax.nn.softmax(x, axis=axis)

def _gelu(x):
    return jax.nn.gelu(x, approximate=True)

def _silu(x):
    return jax.nn.silu(x)

def _sigmoid(x):
    return jax.nn.sigmoid(x)

def _layernorm(x, axis=-1, eps=1e-05):
    m = jnp.mean(x, axis=axis, keepdims=True)
    v = jnp.var(x, axis=axis, keepdims=True)
    return (x - m) / jnp.sqrt(v + eps)

def _scatter_add(tgt, idx, src, axis=0):
    return tgt.at[idx].add(src)

def _segment_sum(src, seg, n):
    return jax.ops.segment_sum(src, seg, n)
kernel_name = 'mk_xattn_ffn_d1_seqx_r4_265f0b'

def setup_inputs(seed: int=0):
    np.random.seed(seed)
    _w = jnp.asarray

    def _rec_inputs():
        import jax
        import jax.numpy as jnp
        _rk = jax.random.key(seed)
        x = 7.22e-05 + 1 * jax.random.normal(jax.random.fold_in(_rk, 1), (8, 112, 512), jnp.float32)
        _lenS = 112 - jax.random.randint(jax.random.fold_in(_rk, 7), (8,), 0, max(1, 112 // 4) + 1, jnp.int32)
        _lenS2 = 375 - jax.random.randint(jax.random.fold_in(_rk, 8), (8,), 0, max(1, 375 // 4) + 1, jnp.int32)
        _ctx_512P = jax.random.normal(jax.random.fold_in(_rk, 11), (8, 16, 128), jnp.float32)
        _ctx_512c = jax.random.dirichlet(jax.random.fold_in(_rk, 511), 0.3 * jnp.ones((16,), jnp.float32), (8, 375))
        _ctx_512t = jnp.einsum('bsk,bkd->bsd', _ctx_512c, _ctx_512P)
        _ctx_512t = _ctx_512t * jax.lax.rsqrt(jnp.mean(jnp.square(_ctx_512t)) + 1e-12) * 0.953939
        ctx_512 = -0.000514642 + 1.00011 * (_ctx_512t + 0.3 * jax.random.normal(jax.random.fold_in(_rk, 611), (8, 375, 128), jnp.float32))
        return (x, ctx_512)
    x, ctx_512 = _rec_inputs()

    def _L0_xattn_setup():
        import jax, jax.numpy as jnp
        import numpy as np
        B, S, H, NH, L = (2, 512, 512, 16, 128)
        HD = H // NH
        key = jax.random.key(seed)
        k1, k2, k3, k4, k5 = jax.random.split(key, 5)
        scale = 0.02
        return {'q': jax.random.normal(k1, (B, S, H), dtype=jnp.float32), 'latent_kv': jax.random.normal(k2, (B, S, L), dtype=jnp.float32), 'Wq': jax.random.normal(k3, (H, H), dtype=jnp.float32) * scale, 'Wkv_expand': jax.random.normal(k4, (2 * H, L), dtype=jnp.float32) * scale, 'Wout': jax.random.normal(k5, (H, H), dtype=jnp.float32) * scale}
    _L0_xattn_all = _L0_xattn_setup()
    _L0_xattn_in = {k: v for k, v in _L0_xattn_all.items() if k in ('Wq', 'Wkv_expand', 'Wout')}
    del _L0_xattn_all

    def _L0_ffn_setup():
        import jax, jax.numpy as jnp
        import numpy as np
        TOP_K = 2
        key = jax.random.key(seed)
        ks = jax.random.split(key, 6)
        B, S, H, F, E = (1, 512, 512, 352, 8)
        Fs = 2 * F
        std = jnp.float32(0.02)
        return {'hidden_states': jax.random.normal(ks[0], (B, S, H), jnp.float32), 'gate_weight': jax.random.normal(ks[1], (E, H), jnp.float32) * std, 'gate_up_weights': jax.random.normal(ks[2], (E, 2 * F, H), jnp.float32) * std, 'down_weights': jax.random.normal(ks[3], (E, H, F), jnp.float32) * std, 'shared_gate_up': jax.random.normal(ks[4], (2 * Fs, H), jnp.float32) * std, 'shared_down': jax.random.normal(ks[5], (H, Fs), jnp.float32) * std}
    _L0_ffn_all = _L0_ffn_setup()
    _L0_ffn_in = {k: v for k, v in _L0_ffn_all.items() if k in ('gate_weight', 'gate_up_weights', 'down_weights', 'shared_gate_up', 'shared_down')}
    del _L0_ffn_all
    return {'x': x, 'ctx_512': ctx_512, 'L0_xattn_Wq': _L0_xattn_in['Wq'], 'L0_xattn_Wkv_expand': _L0_xattn_in['Wkv_expand'], 'L0_xattn_Wout': _L0_xattn_in['Wout'], 'L0_ffn_gate_weight': _L0_ffn_in['gate_weight'], 'L0_ffn_gate_up_weights': _L0_ffn_in['gate_up_weights'], 'L0_ffn_down_weights': _L0_ffn_in['down_weights'], 'L0_ffn_shared_gate_up': _L0_ffn_in['shared_gate_up'], 'L0_ffn_shared_down': _L0_ffn_in['shared_down']}

def reference(x, ctx_512, L0_xattn_Wq, L0_xattn_Wkv_expand, L0_xattn_Wout, L0_ffn_gate_weight, L0_ffn_gate_up_weights, L0_ffn_down_weights, L0_ffn_shared_gate_up, L0_ffn_shared_down):
    import jax
    import jax.numpy as jnp

    def _L0_xattn_ref(q, latent_kv, Wq, Wkv_expand, Wout):
        import jax, jax.numpy as jnp
        import numpy as np
        B, S, H, NH, L = (2, 512, 512, 16, 128)
        HD = H // NH
        b, sq, _ = q.shape
        sk = latent_kv.shape[1]
        qp = q @ Wq.T
        kv = latent_kv @ Wkv_expand.T
        k, v = jnp.split(kv, 2, axis=-1)
        qh = qp.reshape(b, sq, NH, HD).transpose(0, 2, 1, 3)
        kh = k.reshape(b, sk, NH, HD).transpose(0, 2, 1, 3)
        vh = v.reshape(b, sk, NH, HD).transpose(0, 2, 1, 3)
        inv_sqrt_d = 1.0 / jnp.sqrt(jnp.float32(HD))
        scores = jnp.einsum('bhqd,bhkd->bhqk', qh, kh) * inv_sqrt_d
        causal = jnp.tril(jnp.ones((sq, sk), dtype=bool))
        scores = jnp.where(causal, scores, jnp.finfo(scores.dtype).min)
        attn = jax.nn.softmax(scores, axis=-1)
        out = jnp.einsum('bhqk,bhkd->bhqd', attn, vh)
        out = out.transpose(0, 2, 1, 3).reshape(b, sq, H)
        return out @ Wout.T

    def _L0_ffn_ref(hidden_states, gate_weight, gate_up_weights, down_weights, shared_gate_up, shared_down):
        import jax, jax.numpy as jnp
        import numpy as np
        TOP_K = 2
        B, S, H = hidden_states.shape
        E, twoF, _ = gate_up_weights.shape
        F = twoF // 2
        T = B * S
        x = hidden_states.reshape(T, H)
        logits = x @ gate_weight.T
        scores = jax.nn.softmax(logits, axis=-1)
        topk_w, topk_idx = jax.lax.top_k(scores, TOP_K)
        combine = jnp.zeros((T, E), x.dtype).at[jnp.arange(T)[:, None], topk_idx].add(topk_w)
        gu = jnp.einsum('th,efh->tef', x, gate_up_weights)
        act = jax.nn.silu(gu[..., :F]) * gu[..., F:]
        y = jnp.einsum('tef,te,ehf->th', act, combine, down_weights)
        Fs = shared_gate_up.shape[0] // 2
        sgu = x @ shared_gate_up.T
        sact = jax.nn.silu(sgu[:, :Fs]) * sgu[:, Fs:]
        y = y + sact @ shared_down.T
        return y.reshape(B, S, H)
    x = x + _L0_xattn_ref(_layernorm(x, axis=-1), ctx_512, L0_xattn_Wq, L0_xattn_Wkv_expand, L0_xattn_Wout)
    x = x + _L0_ffn_ref(_layernorm(x, axis=-1), L0_ffn_gate_weight, L0_ffn_gate_up_weights, L0_ffn_down_weights, L0_ffn_shared_gate_up, L0_ffn_shared_down)
    return x

_drawn_inputs = setup_inputs


def setup_inputs(seed=0):
    import zlib

    import numpy as np

    out = dict(_drawn_inputs(seed))
    spreads = {}
    factors = {'L0_xattn_Wq': 8.0,
     'L0_ffn_gate_weight': 5.505,
     'L0_ffn_gate_up_weights': 4.622,
     'L0_ffn_down_weights': 4.645,
     'L0_ffn_shared_gate_up': 3.661,
     'L0_ffn_shared_down': 3.662}
    for name, (base, spread) in spreads.items():
        noise = np.random.default_rng([zlib.crc32(name.encode()), seed]).standard_normal(out[name].shape)
        drawn = base * np.exp(spread * noise) if base else spread * noise
        out[name] = jnp.asarray(drawn.astype(out[name].dtype))
    for name, factor in factors.items():
        out[name] = (out[name] * factor).astype(out[name].dtype)
    return out
```

```python
import numpy as np
import concourse.bass as bass
from concourse import mybir
from concourse.alu_op_type import AluOpType as ALU

ACT = mybir.ActivationFunctionType
F32 = mybir.dt.float32
U32 = mybir.dt.uint32
I32 = mybir.dt.int32
F32R = mybir.dt.float32r
AX = mybir.AxisListType

P = 128
LN_EPS = 1e-5
MASKED = -3.0e38


class SbufMap:

    def __init__(self, nc):
        self.nc = nc
        self.at = -(-nc.sbuf_base // 32) * 32

    def region(self, nbytes):
        start, self.at = self.at, self.at + -(-nbytes // 32) * 32
        assert self.at <= self.nc.sbuf_usable_end, self.at
        return start

    def tensor(self, name, shape, dtype=F32):
        return self.inside([self.region(4 * int(np.prod(shape[1:]))), None], name, shape, dtype)

    def inside(self, cursor, name, shape, dtype=F32):
        nbytes = -(-4 * int(np.prod(shape[1:])) // 32) * 32
        t = self.nc.alloc_sbuf_tensor_at(name, shape, dtype, offset=cursor[0])
        cursor[0] += nbytes
        assert cursor[1] is None or cursor[0] <= cursor[1], name
        return t


def build(nc, x, ctxT, wqT, wkvT, woT, gateT, guT, dnT, sguT, sdnT, out):
    NB, SQ, H = x.shape
    L = ctxT.shape[0]
    C = H // P
    HD = 32
    NH = H // HD
    R = P // HD
    E = guT.shape[0]
    F = dnT.shape[1]
    FS = sdnT.shape[0]
    T = NB * SQ
    TOPK = 2
    NT = (TOPK * T + E * (P - 1)) // P
    FK = [(k, min(P, F - k)) for k in range(0, F, P)]
    FSK = [(k, min(P, FS - k)) for k in range(0, FS, P)]
    NQ = 4
    TQ = T // NQ
    BQ = NB // NQ
    SCALE = float(np.float32(1.0) / np.sqrt(np.float32(HD)))
    assert L == P and NT == 21 and NB == 8 and R == 4 and TQ == BQ * SQ

    m = SbufMap(nc)
    GU, DN = C * 2 * F, len(FK) * H
    w_exp_at = m.region(4 * E * (GU + DN))
    w_gu = nc.alloc_sbuf_tensor_at("w_gu", [P, E * GU], F32, offset=w_exp_at)
    w_dn = nc.alloc_sbuf_tensor_at("w_dn", [P, E * DN], F32, offset=w_exp_at + 4 * E * GU)
    w_shared_at = m.region(4 * (C * 2 * FS + len(FSK) * H))
    shared = [w_shared_at, m.at]
    w_sgu = m.inside(shared, "w_sgu", [P, C, 2 * FS])
    att2 = list(shared)
    w_sdn = m.inside(shared, "w_sdn", [P, len(FSK), H])
    xres = m.tensor("xres", [SQ, NB, H])
    x2nT_at = m.region(4 * C * T)
    x2nT = nc.alloc_sbuf_tensor_at("x2nT", [P, C, T], F32, offset=x2nT_at)
    ident = m.tensor("ident", [P, P])
    w_gate = m.tensor("w_gate", [P, C, E])
    small = [m.at, nc.sbuf_usable_end]

    BLK = 4
    NBLK = NB // BLK
    W = BLK * SQ
    att = [w_exp_at, w_shared_at]

    def loaded_and_split(name, shape):
        at = att[0]
        raw = m.inside(att, name, shape)
        lo = nc.alloc_sbuf_tensor_at(name + "_lo", shape, F32R, offset=at)
        return raw, (m.inside(att, name + "_hi", shape, F32R), lo)

    w_q, w_q2 = loaded_and_split("w_q", [P, C, H])
    w_kv, w_kv2 = loaded_and_split("w_kv", [P, 2 * H])
    w_o, w_o2 = loaded_and_split("w_o", [P, C, H])
    ctx, ctx2 = loaded_and_split("ctx", [P, NB, SQ])
    mask = m.inside(att, "mask", [SQ, C, SQ])
    xn = [m.inside(att, f"xn{i}", [SQ, H]) for i in range(2)]
    xnT = (m.inside(att, "xnT_hi", [P, C, W], F32R), m.inside(att, "xnT_lo", [P, C, W], F32R))
    qT = [m.inside(att, f"qT{i}", [P, C, W]) for i in range(NBLK)]
    kT = [m.inside(att, f"kT{i}", [P, C, W]) for i in range(NBLK)]
    v_sb = m.inside(att, "v_sb", [SQ, H])
    score = [m.inside(att2, f"score{r}", [SQ, C, SQ]) for r in range(R)]
    prob = [m.inside(att, f"prob{r}", [SQ, C, SQ]) for r in range(R)]
    probT = [m.inside(att, f"probT{r}", [SQ, C, SQ]) for r in range(R)]
    oT = (m.inside(att2, "oT_hi", [P, C, SQ], F32R), m.inside(att2, "oT_lo", [P, C, SQ], F32R))
    keep = [att[0], w_shared_at]
    keep_from = keep[0]
    x2n = m.inside(keep, "x2n", [SQ, H])
    x2n_all = m.inside(keep, "x2n_all", [SQ, NB, H])
    loop = [x2nT_at, x2nT_at + 4 * C * T]
    xsT = m.inside(loop, "xsT", [P, C, P])
    silu_e = m.inside(loop, "silu_e", [P, F])
    act_e = m.inside(loop, "act_e", [P, F])
    actT_e = m.inside(loop, "actT_e", [P, len(FK), P])
    y_sb = m.inside(loop, "y_sb", [P, H])
    gath = [w_shared_at, m.at]
    y_tok = m.inside(gath, "y_tok", [SQ, NB, TOPK, H])

    sb = lambda name, shape, dtype=F32: m.inside(small, name, shape, dtype)
    silu_s = [sb(f"silu_s{i}", [P, TQ]) for i in range(2)]
    actT_s = sb("actT_s", [P, len(FSK), TQ])
    xs_in = sb("xs_in", [P, H])
    zeros = xs_in
    negmax = sb("negmax", [SQ, R, C])
    rowsum = sb("rowsum", [SQ, R, C])
    rrow = sb("rrow", [SQ, R, C])
    bn1, mv1, var1, rstd1 = (sb(n, [SQ, NB, k]) for n, k in (("bn1", 6), ("mv1", 2), ("var1", 1), ("rstd1", 1)))
    bn2, mv2, var2, rstd2 = (sb(n, [SQ, NB, k]) for n, k in (("bn2", 6), ("mv2", 2), ("var2", 1), ("rstd2", 1)))
    minus_half = sb("minus_half", [SQ, 1])
    sb = lambda name, shape, dtype=F32: m.inside(keep, name, shape, dtype)
    tri = sb("tri", [SQ, SQ])
    ones = sb("ones", [SQ, P])
    down8 = sb("down8", [SQ, NB, E])
    below = sb("below", [P, E, E])
    thresh = sb("thresh", [P, E, T // P])
    tile_no = sb("tile_no", [1, NT, E])
    rt = lambda name: sb(name, [SQ, NB, E])
    logit, pexp, prb, eq, cand, oh1, oh2, prb2 = (rt(n) for n in "logit pexp prb eq cand oh1 oh2 prb2".split())
    rv = lambda name: sb(name, [SQ, NB])
    lmax, lsum, lrec, first1, first2 = (rv(n) for n in "lmax lsum lrec first1 first2".split())
    topw = m.inside(small, "topw", [SQ, TOPK, NB])
    picked = sb("picked", [SQ, NB + 1, E])
    before = sb("before", [SQ, NB + 1, E])
    count = sb("count", [P, E])
    overs = sb("over", [P, E, T // P])
    tiles = sb("tiles", [P, E])
    tilesb = sb("tilesb", [P, E, E])
    base = sb("base", [P, E])
    slot = rt("slot")
    slot1 = rt("slot1")
    slot2 = rt("slot2")
    slot_i = m.inside(small, "slot_i", [SQ, TOPK, NB], U32)
    started = sb("started", [1, NT, E])
    eid_f = sb("eid_f", [1, NT])
    eid = m.inside(small, "eid", [1, NT], I32)

    bank = [nc.alloc_psum_tensor(f"bank{i}", [P, 512], F32) for i in range(8)]
    S = bank[0:4]
    A, B, CC, D = bank[4:8]

    xs_dram = nc.dram_tensor("xs_dram", [NT * P, H], F32, kind="Internal")
    ys_dram = nc.dram_tensor("ys_dram", [NT * P, H], F32, kind="Internal")

    names = (
        "x0 xrest wq wkv wo wgate ctx sgu sdnw we "
        "const zt sel zero "
        "ctx_hi ctx_lo wkv_hi wkv_lo wq_hi wq_lo wo_hi wo_lo "
        "bs1 st1 rs1a rs1b xn T1 xnT_hi xnT_lo Q QT K KT V Vs "
        "S ms mask exp rr prob PT probT O oT_hi oT_lo "
        "op x1 bs2 st2 rs2a rs2b x2n cp T2 x2T "
        "lg rt rtc lexp trip rank pos scat "
        "sg ssil sact sdn sres "
        "xin Tx xsT eg esil eact Ta aT edn ey yst fin out").split()
    s = {n: nc.alloc_semaphore(f"s_{n}") for n in names}
    s_gat = [nc.alloc_semaphore(f"s_gat{b}") for b in range(NB)]

    def chunked(b, n=H):
        return b[0:SQ, 0:n]

    def wait_alone(eng, sem, value):
        eng.wait_ge(sem, value)
        eng.nop(nofuse=True)

    with nc.Block() as block:

        @block.sync
        def _(sp):
            sp.dma_start(ctx[:, :, :], ctxT[:, :, 0:SQ]).then_inc(s["ctx"], 16)
            sp.dma_start(xres[:, 0, :], x[0]).then_inc(s["x0"], 16)
            sp.dma_start(w_kv[:, :], wkvT).then_inc(s["wkv"], 16)
            sp.dma_start(xres[:, 1:NB, :], x[1:NB].rearrange("b q d -> q b d")).then_inc(s["xrest"], 16)
            sp.dma_start(w_q[:, :, :], wqT.rearrange("(c p) d -> p c d", p=P)).then_inc(s["wq"], 16)
            sp.dma_start(w_o[:, :, :], woT.rearrange("(c p) d -> p c d", p=P)).then_inc(s["wo"], 16)
            sp.dma_start(w_gate[:, :, :], gateT).then_inc(s["wgate"], 16)
            sp.wait_ge(s["zt"], 1)
            sp.dma_start(xs_dram[:, :].rearrange("(n p) d -> p n d", p=P),
                         zeros[:, :].unsqueeze(1).to_broadcast([P, NT, H])).then_inc(s["zero"], 16)
            sp.dma_start(w_sgu[:, :, :], sguT).then_inc(s["sgu"], 16)

            def load_gu(e, sem):
                sp.dma_start(w_gu[:, e * GU:(e + 1) * GU], guT[e].rearrange("p c f -> p (c f)")).then_inc(sem, 16)

            def load_dn(e, sem):
                k2 = F // P * P
                at = w_dn[:, e * DN:(e + 1) * DN].rearrange("p (k d) -> p k d", d=H)
                sp.dma_start(at[:, 0:k2 // P, :],
                             dnT[e, 0:k2, :].rearrange("(k p) d -> p k d", p=P)).then_inc(sem, 16)
                sp.dma_start(at[0:F - k2, k2 // P, :], dnT[e, k2:F, :]).then_inc(sem, 16)

            n_early = sum(w_exp_at + 4 * (E * GU + (e + 1) * DN) <= keep_from for e in range(E))
            sp.wait_ge(s["op"], NB)
            whole = FS // P * P
            sp.dma_start(w_sdn[:, 0:whole // P, :],
                         sdnT[0:whole, :].rearrange("(k p) d -> p k d", p=P)).then_inc(s["sdnw"], 16)
            sp.dma_start(w_sdn[0:FS - whole, whole // P, :], sdnT[whole:FS, :]).then_inc(s["sdnw"], 16)
            for e in range(E):
                load_gu(e, s["we"])
            for e in range(n_early):
                load_dn(e, s["we"])
            sp.wait_ge(s["pos"], 3)
            sp.wait_ge(s["scat"], 16 * TOPK * NB)
            for e in range(n_early, E):
                load_dn(e, s["we"])

            def load_x(i):
                sp.dma_start(xs_in[:, :], xs_dram[bass.ds(i * P, P), :]).then_inc(s["xin"], 16)

            def store_y(i):
                sp.dma_start(ys_dram[bass.ds(i * P, P), :], y_sb[:, :]).then_inc(s["yst"], 16)

            load_x(0)
            sp.wait_ge(s["Tx"], 1)
            load_x(1)
            with sp.Fori(1, NT - 1) as i:
                sp.wait_ge(s["Tx"], i + 1)
                load_x(i + 1)
                sp.wait_ge(s["ey"], i)
                store_y(i - 1)
            for i in (NT - 2, NT - 1):
                sp.wait_ge(s["ey"], i + 1)
                store_y(i)
            for b in range(NB):
                sp.wait_ge(s["fin"], b + 1)
                sp.dma_start(out[b], xres[:, b, :]).then_inc(s["out"], 16)
            sp.wait_ge(s["out"], 16 * NB)

        @block.gpsimd
        def _(pool):
            cnt = [0]

            def own(ins):
                cnt[0] += 1
                ins.then_inc(s["sel"], 1)
                pool.wait_ge(s["sel"], cnt[0])

            own(pool.memset(ident[:, :], 0.0))
            pool.affine_select(out=ident[:, :], in_=ident[:, :], compare_op=ALU.not_equal, fill=1.0, base=0,
                               pattern=[[-1, P]], channel_multiplier=1).then_inc(s["const"], 1)
            pool.memset(minus_half[:, :], -0.5).then_inc(s["const"], 1)
            pool.memset(zeros[:, :], 0.0).then_inc(s["zt"], 1)
            own(pool.memset(mask[:, :, :], 0.0))
            pool.affine_select(out=mask[:, :, :], in_=mask[:, :, :], compare_op=ALU.is_ge, fill=MASKED, base=0,
                               pattern=[[0, C], [-1, SQ]], channel_multiplier=1).then_inc(s["const"], 1)
            pool.wait_ge(s["const"], 3)

            def rstd(n, stats, var, rs, mv, own_sem, done):
                pool.wait_ge(s[stats], n + 1)
                pool.tensor_scalar(var[:, n, :], mv[:, n, 1:2], LN_EPS, 1.0, ALU.add, ALU.mult).then_inc(s[own_sem], 1)
                pool.wait_ge(s[own_sem], n + 1)
                pool.tensor_tensor(rs[:, n, :], var[:, n, :], minus_half[:, :], ALU.pow).then_inc(s[done], 1)

            for n in range(NB):
                rstd(n, "st1", var1, rstd1, mv1, "rs1a", "rs1b")
            pool.wait_ge(s["wo"], 16)
            pool.tensor_copy(w_o2[0][:, :, :], w_o[:, :, :]).then_inc(s["wo_hi"], 1)
            pool.wait_ge(s["wo_hi"], 1)
            pool.tensor_tensor(w_o2[1][:, :, :], w_o[:, :, :], w_o2[0][:, :, :].bitcast(F32), ALU.subtract)\
                .then_inc(s["wo_lo"], 1)
            own(pool.memset(tri[:, :], 1.0))
            own(pool.affine_select(out=tri[:, :], in_=tri[:, :], compare_op=ALU.is_gt, fill=0.0, base=0,
                                   pattern=[[1, SQ]], channel_multiplier=-1))
            own(pool.memset(ones[:, :], 1.0))
            own(pool.iota(down8[:, :, :], [[0, NB], [-1, E]], base=E, channel_multiplier=0,
                          allow_small_or_imprecise_dtypes=True))
            own(pool.memset(below[:, :, :], 1.0))
            own(pool.affine_select(out=below[:, :, :], in_=below[:, :, :], compare_op=ALU.is_gt, fill=0.0, base=0,
                                   pattern=[[1, E], [-1, E]], channel_multiplier=0))
            own(pool.iota(thresh[:, :, :], [[0, E], [P, T // P]], base=0, channel_multiplier=0,
                          allow_small_or_imprecise_dtypes=True))
            own(pool.iota(tile_no[:, :, :], [[1, NT], [0, E]], base=0, channel_multiplier=0,
                          allow_small_or_imprecise_dtypes=True))
            pool.memset(before[:, 0:1, :], 0.0).then_inc(s["const"], 1)
            for n in range(NB):
                rstd(n, "st2", var2, rstd2, mv2, "rs2a", "rs2b")
                pool.wait_ge(s["x2n"], n + 1)
                pool.tensor_copy(x2n_all[:, n, :], x2n[:, :]).then_inc(s["cp"], 1)

            pool.wait_ge(s["zero"], 16)
            pool.wait_ge(s["cp"], NB)
            pool.wait_ge(s["pos"], 2)
            for b in range(NB):
                for k in range(TOPK):
                    pool.indirect_dma_start(
                        out=xs_dram[:, :], out_offset=bass.IndirectOffsetOnAxis(ap=slot_i[:, k, b:b + 1], axis=0),
                        in_=x2n_all[:, b, :], in_offset=None).then_inc(s["scat"], 16)
            pool.wait_ge(s["yst"], 16 * NT)
            for b in range(NB):
                for k in range(TOPK):
                    pool.indirect_dma_start(
                        out=y_tok[:, b, k, :], out_offset=None, in_=ys_dram[:, :],
                        in_offset=bass.IndirectOffsetOnAxis(ap=slot_i[:, k, b:b + 1], axis=0)).then_inc(s_gat[b], 16)

        @block.tensor
        def _(pe):
            def transposes(dst, src):
                for c in range(C):
                    ins = pe.transpose(dst[:, c * SQ:(c + 1) * SQ], src[:, c * P:(c + 1) * P], ident[0:SQ, 0:SQ])
                return ins

            def product(dst, terms, start=True, stop=True):
                passes = [(a[i], b[j]) for a, b in terms for i, j in ((1, 0), (0, 1), (0, 0))]
                for n, (a, b) in enumerate(passes):
                    ins = pe.matmul(dst, a, b, start=start and n == 0, stop=stop and n == len(passes) - 1)
                return ins

            def both(pair, *at):
                return tuple(t[at] for t in pair)

            every = slice(None)

            def t1(n, bank_):
                pe.wait_ge(s["xn"], n + 1)
                transposes(bank_, xn[n % 2]).then_inc(s["T1"], 1)

            def q_proj(k, j, bank_):
                product(bank_[:, 0:W], [(both(w_q2, every, c, slice(j * P, (j + 1) * P)), both(xnT, every, c, every))
                                        for c in range(C)]).then_inc(s["Q"], 1)

            def k_proj(k, j, bank_):
                product(bank_[:, 0:W], [(both(w_kv2, every, slice(j * P, (j + 1) * P)),
                                         both(ctx2, every, slice(k * BLK, (k + 1) * BLK), every))]).then_inc(s["K"], 1)

            def v_proj(n):
                product(A[0:SQ, :], [(both(ctx2, every, n, every), both(w_kv2, every, slice(H, 2 * H)))])\
                    .then_inc(s["V"], 1)

            def out_proj(n, first, last):
                pe.wait_ge(s["oT_hi"], n + 1)
                pe.wait_ge(s["oT_lo"], n + 1)
                ins = product(D[0:SQ, :], [(both(oT, every, c, every), both(w_o2, every, c, every))
                                           for c in range(first, last)], first == 0, last == C)
                if last == C:
                    ins.then_inc(s["op"], 1)

            def t2(n):
                pe.wait_ge(s["x2n"], n + 1)
                transposes(B, x2n).then_inc(s["T2"], 1)

            def scores(b):
                k, cols = b // BLK, slice(b % BLK * SQ, (b % BLK + 1) * SQ)
                pe.wait_ge(s["QT"], C * (k + 1))
                pe.wait_ge(s["KT"], C * (k + 1))
                for c in range(C):
                    for r in range(R):
                        rows = slice(HD * r, HD * (r + 1))
                        ins = pe.matmul(S[r][0:SQ, c * SQ:(c + 1) * SQ], qT[k][rows, c, cols], kT[k][rows, c, cols],
                                        start=True, stop=True)
                        if c == C - 1:
                            ins.then_inc(s["S"], 1)

            pe.wait_ge(s["const"], 3)
            for what in ("ctx_hi", "ctx_lo", "wkv_hi", "wkv_lo"):
                pe.wait_ge(s[what], 1)
            for j in range(C):
                k_proj(0, j, bank[4 + j])
            for n in range(BLK):
                t1(n, S[n])
            for what, value in (("wq_hi", 1), ("wq_lo", 1), ("xnT_hi", BLK), ("xnT_lo", BLK)):
                pe.wait_ge(s[what], value)
            for j in range(C):
                pe.wait_ge(s["KT"], j + 1)
                q_proj(0, j, bank[4 + j])
            scores(0)
            for n in range(BLK, NB):
                pe.wait_ge(s["QT"], n - BLK + 1)
                t1(n, bank[n])
            pe.wait_ge(s["xnT_hi"], BLK + 1)
            pe.wait_ge(s["xnT_lo"], BLK + 1)
            v_proj(0)
            pe.wait_ge(s["xnT_hi"], NB)
            pe.wait_ge(s["xnT_lo"], NB)

            def fill(j):
                q_proj(1, j, D)
                k_proj(1, j, CC)

            fill(0)
            for b in range(NB):
                if b + 1 < NB:
                    pe.wait_ge(s["mask"], R * (b + 1))
                    scores(b + 1)
                if b >= 2:
                    t2(b - 2)
                if 1 <= b + 1 < C:
                    pe.wait_ge(s["QT"], C + b + 1)
                    if b >= 2:
                        pe.wait_ge(s["x1"], b - 1)
                    pe.wait_ge(s["KT"], C + b + 1)
                    if b >= 1:
                        pe.wait_ge(s["oT_hi"], b)
                        pe.wait_ge(s["oT_lo"], b)
                    fill(b + 1)
                for r in range(R):
                    pe.wait_ge(s["prob"], R * b + r + 1)
                    if r == 0:
                        pe.wait_ge(s["Vs"], b + 1)
                    if r == 1 and b >= 2:
                        pe.wait_ge(s["x2T"], b - 1)
                    if r >= 2:
                        pe.wait_ge(s["probT"], R * b + r - 1)
                    for c in range(C):
                        ins = pe.transpose((A, B)[r % 2][0:SQ, c * SQ:(c + 1) * SQ], prob[r][:, c, :],
                                           ident[0:SQ, 0:SQ])
                    ins.then_inc(s["PT"], 1)
                    if b >= 1 and r == 1:
                        pe.wait_ge(s["QT"], C * NBLK if b >= C - 1 else C + b + 2)
                        if b >= 2:
                            pe.wait_ge(s["x1"], b - 1)
                        if b == 1:
                            pe.wait_ge(s["wo_hi"], 1)
                            pe.wait_ge(s["wo_lo"], 1)
                        out_proj(b - 1, 0, C // 2)
                    if b >= 1 and r == 3:
                        out_proj(b - 1, C // 2, C)
                pe.wait_ge(s["KT"], C * NBLK if b >= C - 1 else C + b + 2)
                for h in range(NH):
                    r, c = h % R, h // R
                    if c == 0:
                        pe.wait_ge(s["probT"], R * b + r + 1)
                    ins = pe.matmul(CC[HD * r:HD * (r + 1), c * SQ:(c + 1) * SQ], v_sb[:, h * HD:(h + 1) * HD],
                                    probT[r][:, c, :], start=True, stop=True)
                ins.then_inc(s["O"], 1)
                if b + 1 < NB:
                    v_proj(b + 1)
            t2(NB - 2)
            pe.wait_ge(s["x1"], NB - 1)
            out_proj(NB - 1, 0, C)

            def shared_block(q):
                for j, (k, w) in enumerate(FSK):
                    n = len(FSK) * q + j
                    G, U = S[j % 2], S[2 + j % 2]
                    if j >= 2:
                        wait_alone(pe, s["sact"], n - 1)
                    for dst, f0 in ((G, k), (U, FS + k)):
                        for c in range(C):
                            ins = pe.matmul(dst[0:w, 0:TQ], w_sgu[:, c, f0:f0 + w], x2nT[:, c, bass.ds(q * TQ, TQ)],
                                            start=c == 0, stop=c == C - 1)
                    ins.then_inc(s["sg"], 1)
                pe.wait_ge(s["sdnw"], 32)
                for t in range(BQ):
                    dst = (A, D)[t]
                    for j, (k, w) in enumerate(FSK):
                        if t == 0:
                            pe.wait_ge(s["sact"], len(FSK) * q + j + 1)
                        ins = pe.matmul(dst[0:SQ, :], actT_s[0:w, j, t * SQ:(t + 1) * SQ], w_sdn[0:w, j, :],
                                        start=j == 0, stop=j == len(FSK) - 1)
                    ins.then_inc(s["sdn"], 1)

            pe.wait_ge(s["sgu"], 16)
            pe.wait_ge(s["mask"], R * NB)
            pe.wait_ge(s["x2T"], NB - 1)
            pe.wait_ge(s["x1"], NB)
            t2(NB - 1)
            shared_block(0)
            pe.wait_ge(s["x2T"], NB)
            pe.wait_ge(s["wgate"], 16)
            for b in range(NB):
                for c in range(C):
                    ins = pe.matmul(B[0:SQ, b * E:(b + 1) * E], x2nT[:, c, b * SQ:(b + 1) * SQ], w_gate[:, c, :],
                                    start=c == 0, stop=c == C - 1)
            ins.then_inc(s["lg"], 1)
            pe.wait_ge(s["sres"], BQ)
            shared_block(1)
            pe.wait_ge(s["trip"], 1)
            pe.matmul(B[0:SQ, 0:NB * E], tri[:, :], picked[:, 0:NB, :], start=True, stop=False)
            pe.matmul(B[0:SQ, 0:NB * E], ones[:, 0:SQ], before[:, 0:NB, :], start=False, stop=True).then_inc(s["rank"], 1)
            pe.matmul(CC[:, 0:E], ones[:, :], before[:, NB, :], start=True, stop=True).then_inc(s["rank"], 1)
            with pe.Fori(2, NQ) as q:
                pe.wait_ge(s["sres"], BQ * q)
                shared_block(q)

            def gate_up(i):
                pe.wait_ge(s["xsT"], i + 1)
                e = pe.value_load(eid[0:1, bass.ds(i, 1)], min_val=0, max_val=E - 1)
                for dst, f0 in ((S[0], 0), (S[1], F)):
                    for c in range(C):
                        ins = pe.matmul(dst[:, 0:F], xsT[:, c, :], w_gu[:, bass.ds(e * GU + (c * 2 * F + f0), F)],
                                        start=c == 0, stop=c == C - 1)
                    ins.then_inc(s["eg"], 1)

            def t_x(i):
                pe.wait_ge(s["xin"], 16 * i + 16)
                for c in range(C):
                    ins = pe.transpose(S[2][:, c * P:(c + 1) * P], xs_in[:, c * P:(c + 1) * P], ident[:, :])
                ins.then_inc(s["Tx"], 1)

            def down(i):
                pe.wait_ge(s["aT"], i + 1)
                e = pe.value_load(eid[0:1, bass.ds(i, 1)], min_val=0, max_val=E - 1)
                for j, (k, w) in enumerate(FK):
                    ins = pe.matmul(A[:, :], actT_e[0:w, j, :], w_dn[0:w, bass.ds(e * DN + j * H, H)],
                                    start=j == 0, stop=j == len(FK) - 1)
                ins.then_inc(s["edn"], 1)

            def t_act(i):
                pe.wait_ge(s["eact"], i + 1)
                for j, (k, w) in enumerate(FK):
                    ins = pe.transpose(S[3][0:w, j * P:(j + 1) * P], act_e[:, k:k + w], ident[:, :])
                ins.then_inc(s["Ta"], 1)

            pe.wait_ge(s["sres"], NB)
            t_x(0)
            pe.wait_ge(s["pos"], 3)
            pe.wait_ge(s["we"], 16 * 3 * E)
            gate_up(0)
            t_x(1)
            t_act(0)
            gate_up(1)
            t_x(2)
            down(0)
            t_act(1)
            with pe.Fori(2, NT - 1) as i:
                gate_up(i)
                t_x(i + 1)
                pe.wait_ge(s["ey"], i - 1)
                down(i - 1)
                t_act(i)
            gate_up(NT - 1)
            pe.wait_ge(s["ey"], NT - 2)
            down(NT - 2)
            t_act(NT - 1)
            pe.wait_ge(s["ey"], NT - 1)
            down(NT - 1)

        @block.scalar
        def _(act):
            def copy_out(dst, src, sem):
                act.activation(dst, src, ACT.Copy).then_inc(s[sem], 1)

            def as_chunks(b, w=SQ, p=P):
                return b[0:p, 0:C * w].rearrange("p (c q) -> p c q", c=C)

            def hi(dst, src, sem):
                copy_out(dst, src, sem)

            def put_xnT(n, bank_):
                act.wait_ge(s["T1"], n + 1)
                at = n % BLK * SQ
                hi(xnT[0][:, :, at:at + SQ], as_chunks(bank_), "xnT_hi")

            def put_qT(k, j, bank_):
                act.wait_ge(s["Q"], C * k + j + 1)
                copy_out(qT[k][:, j, :], bank_[:, 0:W], "QT")

            def put_kT(k, j, bank_):
                act.wait_ge(s["K"], C * k + j + 1)
                copy_out(kT[k][:, j, :], bank_[:, 0:W], "KT")

            def put_v(n):
                act.wait_ge(s["V"], n + 1)
                copy_out(v_sb[:, :], A[0:SQ, :], "Vs")

            def put_x2T(n):
                act.wait_ge(s["T2"], n + 1)
                copy_out(x2nT[:, :, n * SQ:(n + 1) * SQ], as_chunks(B), "x2T")

            def exps(b, r):
                act.wait_ge(s["mask"], R * b + r + 1)
                if b >= 1:
                    act.wait_ge(s["PT"], R * (b - 1) + r + 1)
                for c in range(C):
                    ins = act.activation(prob[r][:, c, :], score[r][:, c, :], ACT.Exp, bias=negmax[:, r, c:c + 1],
                                         accum_out=rowsum[:, r, c:c + 1])
                ins.then_inc(s["exp"], 1)

            def put_pT(b, r):
                act.wait_ge(s["PT"], R * b + r + 1)
                copy_out(probT[r][:, :, :], as_chunks((A, B)[r % 2], p=SQ), "probT")

            act.wait_ge(s["ctx"], 16)
            hi(ctx2[0][:, :, :], ctx[:, :, :], "ctx_hi")
            act.wait_ge(s["wkv"], 16)
            hi(w_kv2[0][:, :], w_kv[:, :], "wkv_hi")
            for j in range(C):
                put_kT(0, j, bank[4 + j])
            act.wait_ge(s["wq"], 16)
            hi(w_q2[0][:, :, :], w_q[:, :, :], "wq_hi")
            for n in range(BLK):
                put_xnT(n, S[n])
            for j in range(C):
                put_qT(0, j, bank[4 + j])
            for n in range(BLK, NB):
                put_xnT(n, bank[n])
                exps(0, n - BLK)
            put_v(0)
            put_qT(1, 0, D)
            put_kT(1, 0, CC)
            for b in range(NB):
                if 1 <= b + 1 < C:
                    put_qT(1, b + 1, D)
                    put_kT(1, b + 1, CC)
                if b >= 2:
                    put_x2T(b - 2)
                for r in range(0, R, 2):
                    put_pT(b, r)
                    put_pT(b, r + 1)
                    if b + 1 < NB:
                        exps(b + 1, r // 2)
                act.wait_ge(s["O"], b + 1)
                hi(oT[0][:, :, :], as_chunks(CC), "oT_hi")
                if b + 1 < NB:
                    put_v(b + 1)
                    exps(b + 1, 2)
                    exps(b + 1, 3)

            def shared_silu(q):
                for j, (k, w) in enumerate(FSK):
                    act.wait_ge(s["sg"], len(FSK) * q + j + 1)
                    act.activation(silu_s[j % 2][0:w, :], S[j % 2][0:w, 0:TQ], ACT.Silu).then_inc(s["ssil"], 1)

            put_x2T(NB - 2)
            put_x2T(NB - 1)
            shared_silu(0)
            act.wait_ge(s["rt"], 1)
            act.activation(pexp[:, :, :], logit[:, :, :], ACT.Exp).then_inc(s["lexp"], 1)
            shared_silu(1)
            with act.Fori(2, NQ) as q:
                shared_silu(q)

            def put_xsT(i):
                act.wait_ge(s["Tx"], i + 1)
                copy_out(xsT[:, :, :], as_chunks(S[2], w=P), "xsT")

            def silu(i):
                act.wait_ge(s["eg"], 2 * i + 1)
                act.activation(silu_e[:, :], S[0][:, 0:F], ACT.Silu).then_inc(s["esil"], 1)

            def put_y(i, wait=True):
                act.wait_ge(s["edn"], i + 1)
                if wait:
                    act.wait_ge(s["yst"], 16 * i)
                copy_out(y_sb[:, :], A[:, :], "ey")

            act.wait_ge(s["sdn"], NB)
            put_xsT(0)
            silu(0)
            put_xsT(1)
            silu(1)
            put_xsT(2)
            put_y(0, wait=False)
            with act.Fori(2, NT - 1) as i:
                silu(i)
                put_xsT(i + 1)
                put_y(i - 1)
            silu(NT - 1)
            put_y(NT - 2)
            put_y(NT - 1)

        @block.vector
        def _(dve):
            def stats(n, bn, mv, own_sem, done):
                dve.bn_stats(bn[:, n, :], xres[:, n, :]).then_inc(s[own_sem], 1)
                dve.wait_ge(s[own_sem], n + 1)
                dve.bn_aggr(mv[:, n, :], bn[:, n, :]).then_inc(s[done], 1)

            def apply(n, dst, mv, rs, ready, done):
                dve.wait_ge(s[ready], n + 1)
                dve.tensor_scalar(dst[:, :], xres[:, n, :], mv[:, n, 0:1], rs[:, n, :],
                                  ALU.subtract, ALU.mult).then_inc(s[done], 1)

            def lo(parts, src, hi_sem, value, sem, at):
                dve.wait_ge(s[hi_sem], value)
                hi_, lo_ = (t[at] for t in parts)
                dve.tensor_tensor(lo_, src, hi_.bitcast(F32), ALU.subtract).then_inc(s[sem], 1)

            def as_chunks(b):
                return b[:, 0:C * SQ].rearrange("p (c q) -> p c q", c=C)

            def stats1(n):
                stats(n, bn1, mv1, "bs1", "st1")

            def apply1(n):
                if n >= 2:
                    dve.wait_ge(s["T1"], n - 1)
                apply(n, xn[n % 2], mv1, rstd1, "rs1b", "xn")

            def xnT_lo(n, bank_):
                at = n % BLK * SQ
                lo(xnT, as_chunks(bank_), "xnT_hi", n + 1, "xnT_lo", (slice(None), slice(None), slice(at, at + SQ)))

            def add_attention(n):
                dve.wait_ge(s["op"], n + 1)
                dve.tensor_tensor(xres[:, n, :], xres[:, n, :], D[0:SQ, :], ALU.add).then_inc(s["x1"], 1)
                dve.wait_ge(s["x1"], n + 1)
                stats(n, bn2, mv2, "bs2", "st2")

            def apply2(n):
                if n >= 1:
                    dve.wait_ge(s["cp"], n)
                    dve.wait_ge(s["T2"], n)
                apply(n, x2n, mv2, rstd2, "rs2b", "x2n")

            def masked(b, r):
                dve.wait_ge(s["S"], R * b + r + 1)
                dve.scalar_tensor_tensor(out=score[r][:, :, :].rearrange("p c k -> p (c k)"),
                                         in0=S[r][0:SQ, 0:C * SQ], scalar=SCALE,
                                         in1=mask[:, :, :].rearrange("p c k -> p (c k)"),
                                         op0=ALU.mult, op1=ALU.add).then_inc(s["ms"], 1)
                dve.wait_ge(s["ms"], R * b + r + 1)
                dve.tensor_reduce(negmax[:, r, :], score[r][:, :, :], AX.X, ALU.max, negate=True)\
                   .then_inc(s["mask"], 1)

            def normalised(b, r):
                dve.wait_ge(s["exp"], R * b + r + 1)
                dve.reciprocal(rrow[:, r, :], rowsum[:, r, :]).then_inc(s["rr"], 1)
                dve.wait_ge(s["rr"], R * b + r + 1)
                dve.tensor_tensor(prob[r][:, :, :], prob[r][:, :, :],
                                  rrow[:, r, :].unsqueeze(2).to_broadcast([SQ, C, SQ]), ALU.mult)\
                   .then_inc(s["prob"], 1)

            whole = slice(None)
            dve.wait_ge(s["x0"], 16)
            stats1(0)
            dve.wait_ge(s["ctx"], 16)
            lo(ctx2, ctx[:, :, :], "ctx_hi", 1, "ctx_lo", (whole, whole, whole))
            apply1(0)
            dve.wait_ge(s["wkv"], 16)
            lo(w_kv2, w_kv[:, :], "wkv_hi", 1, "wkv_lo", (whole, whole))
            dve.wait_ge(s["xrest"], 16)
            stats1(1)
            stats1(2)
            apply1(1)
            stats1(3)
            apply1(2)
            xnT_lo(0, S[0])
            apply1(3)
            xnT_lo(1, S[1])
            dve.wait_ge(s["wq"], 16)
            lo(w_q2, w_q[:, :, :], "wq_hi", 1, "wq_lo", (whole, whole, whole))
            xnT_lo(2, S[2])
            xnT_lo(3, S[3])
            for n in range(BLK, NB):
                stats1(n)
            apply1(BLK)
            apply1(BLK + 1)
            dve.wait_ge(s["const"], 3)
            masked(0, 0)
            masked(0, 1)
            xnT_lo(BLK, bank[BLK])
            apply1(BLK + 2)
            masked(0, 2)
            xnT_lo(BLK + 1, bank[BLK + 1])
            apply1(BLK + 3)
            masked(0, 3)
            for n in range(BLK + 2, NB):
                xnT_lo(n, bank[n])
            for r in range(R):
                normalised(0, r)
            for b in range(NB):
                if b + 1 < NB:
                    for r in range(R):
                        masked(b + 1, r)
                if b >= 1:
                    add_attention(b - 1)
                if b + 1 < NB:
                    normalised(b + 1, 0)
                    normalised(b + 1, 1)
                if b >= 1:
                    apply2(b - 1)
                lo(oT, as_chunks(CC), "oT_hi", b + 1, "oT_lo", (whole, whole, whole))
                if b + 1 < NB:
                    normalised(b + 1, 2)
                    normalised(b + 1, 3)
            add_attention(NB - 1)
            apply2(NB - 1)

            def shared_act(q):
                for j, (k, w) in enumerate(FSK):
                    dve.wait_ge(s["ssil"], len(FSK) * q + j + 1)
                    dve.tensor_tensor(actT_s[0:w, j, :], S[2 + j % 2][0:w, 0:TQ], silu_s[j % 2][0:w, :], ALU.mult)\
                       .then_inc(s["sact"], 1)
                for t in range(BQ):
                    dve.wait_ge(s["sdn"], BQ * q + t + 1)
                    at = xres[:, bass.ds(q * BQ + t, 1), :].rearrange("q b d -> q (b d)")
                    dve.tensor_tensor(at, at, (A, D)[t][0:SQ, :], ALU.add).then_inc(s["sres"], 1)

            cnt = [0]

            def link(ins):
                cnt[0] += 1
                ins.then_inc(s["rtc"], 1)
                dve.wait_ge(s["rtc"], cnt[0])

            def over_e(v):
                return v.unsqueeze(2).to_broadcast([SQ, NB, E])

            def pick(p, top, first, oh):
                link(dve.tensor_reduce(top, p[:, :, :], AX.X, ALU.max))
                link(dve.tensor_tensor(eq[:, :, :], p[:, :, :], over_e(top), ALU.is_equal))
                link(dve.tensor_tensor(cand[:, :, :], eq[:, :, :], down8[:, :, :], ALU.mult))
                link(dve.tensor_reduce(first[:, :], cand[:, :, :], AX.X, ALU.max))
                link(dve.tensor_tensor(oh[:, :, :], down8[:, :, :], over_e(first[:, :]), ALU.is_equal))

            shared_act(0)
            dve.wait_ge(s["lg"], 1)
            dve.wait_ge(s["const"], 4)
            lg = B[0:SQ, 0:NB * E].rearrange("p (b e) -> p b e", e=E)
            link(dve.tensor_reduce(lmax[:, :], lg, AX.X, ALU.max))
            dve.tensor_tensor(logit[:, :, :], lg, over_e(lmax[:, :]), ALU.subtract).then_inc(s["rt"], 1)
            dve.wait_ge(s["lexp"], 1)
            link(dve.tensor_reduce(lsum[:, :], pexp[:, :, :], AX.X, ALU.add))
            link(dve.reciprocal(lrec[:, :], lsum[:, :]))
            link(dve.tensor_tensor(prb[:, :, :], pexp[:, :, :], over_e(lrec[:, :]), ALU.mult))
            pick(prb, topw[:, 0, :], first1, oh1)
            link(dve.scalar_tensor_tensor(out=prb2[:, :, :], in0=oh1[:, :, :], scalar=-2.0, in1=prb[:, :, :],
                                          op0=ALU.mult, op1=ALU.add))
            pick(prb2, topw[:, 1, :], first2, oh2)
            link(dve.tensor_tensor(picked[:, 0:NB, :], oh1[:, :, :], oh2[:, :, :], ALU.add))
            for b in range(NB):
                last = dve.tensor_tensor(before[:, b + 1, :], before[:, b, :], picked[:, b, :], ALU.add)
                if b < NB - 1:
                    link(last)
            last.then_inc(s["trip"], 1)
            shared_act(1)
            dve.wait_ge(s["rank"], 2)
            link(dve.tensor_copy(count[:, :], CC[:, 0:E]))
            link(dve.tensor_tensor(overs[:, :, :], count[:, :].unsqueeze(2).to_broadcast([P, E, T // P]),
                                   thresh[:, :, :], ALU.is_gt))
            link(dve.tensor_reduce(tiles[:, :], overs[:, :, :], AX.X, ALU.add))
            link(dve.tensor_tensor(tilesb[:, :, :], tiles[:, :].unsqueeze(1).to_broadcast([P, E, E]),
                                   below[:, :, :], ALU.mult))
            link(dve.tensor_reduce(base[:, :], tilesb[:, :, :], AX.X, ALU.add))
            link(dve.scalar_tensor_tensor(out=slot[:, :, :], in0=base[0:SQ, :].unsqueeze(1).to_broadcast([SQ, NB, E]),
                                          scalar=float(P), in1=B[0:SQ, 0:NB * E].rearrange("p (b e) -> p b e", e=E),
                                          op0=ALU.mult, op1=ALU.add))
            link(dve.tensor_tensor(slot1[:, :, :], slot[:, :, :], oh1[:, :, :], ALU.mult))
            link(dve.tensor_tensor(slot2[:, :, :], slot[:, :, :], oh2[:, :, :], ALU.mult))
            with nc.allow_low_precision(reason="slots are whole numbers under 2^24, exact in both types"):
                dve.tensor_reduce(slot_i[:, 0, :], slot1[:, :, :], AX.X, ALU.add).then_inc(s["pos"], 1)
                dve.tensor_reduce(slot_i[:, 1, :], slot2[:, :, :], AX.X, ALU.add).then_inc(s["pos"], 1)
            link(dve.tensor_tensor(started[:, :, :], tile_no[:, :, :], base[0:1, :].unsqueeze(1).to_broadcast([1, NT, E]),
                                   ALU.is_ge))
            link(dve.tensor_reduce(eid_f[:, :], started[:, :, :], AX.X, ALU.add))
            dve.tensor_scalar(eid[:, :], eid_f[:, :], -1.0, None, ALU.add).then_inc(s["pos"], 1)
            with dve.Fori(2, NQ) as q:
                shared_act(q)

            def expert_act(i):
                dve.wait_ge(s["esil"], i + 1)
                dve.wait_ge(s["eg"], 2 * i + 2)
                dve.tensor_tensor(act_e[:, :], S[1][:, 0:F], silu_e[:, :], ALU.mult).then_inc(s["eact"], 1)
                dve.wait_ge(s["Ta"], i + 1)
                whole, rest = F // P, F % P
                dve.tensor_copy(actT_e[:, 0:whole, :], S[3][:, 0:whole * P].rearrange("p (k t) -> p k t", k=whole))
                dve.tensor_copy(actT_e[0:rest, whole, :], S[3][0:rest, whole * P:(whole + 1) * P]).then_inc(s["aT"], 1)

            expert_act(0)
            with dve.Fori(1, NT) as i:
                expert_act(i)

            for b in range(NB):
                dve.wait_ge(s_gat[b], 16 * TOPK)
                link(dve.scalar_tensor_tensor(out=xres[:, b, :], in0=y_tok[:, b, 0, :], scalar=topw[:, 0, b:b + 1],
                                              in1=xres[:, b, :], op0=ALU.mult, op1=ALU.add))
                dve.scalar_tensor_tensor(out=xres[:, b, :], in0=y_tok[:, b, 1, :], scalar=topw[:, 1, b:b + 1],
                                         in1=xres[:, b, :], op0=ALU.mult, op1=ALU.add).then_inc(s["fin"], 1)


def kernel(x, ctx_512, L0_xattn_Wq, L0_xattn_Wkv_expand, L0_xattn_Wout, L0_ffn_gate_weight,
           L0_ffn_gate_up_weights, L0_ffn_down_weights, L0_ffn_shared_gate_up, L0_ffn_shared_down):
    import concourse.bacc as bacc
    from concourse.bass_utils import run_bass_kernel_spmd

    def by_rows(w):
        t = np.swapaxes(np.asarray(w), -1, -2)
        t = t.reshape(*t.shape[:-2], t.shape[-2] // P, P, t.shape[-1])
        return np.swapaxes(t, -3, -2)

    arrays = {
        "x": x,
        "ctxT": np.asarray(ctx_512).transpose(2, 0, 1),
        "wqT": np.asarray(L0_xattn_Wq).T,
        "wkvT": np.asarray(L0_xattn_Wkv_expand).T,
        "woT": np.asarray(L0_xattn_Wout).T,
        "gateT": by_rows(L0_ffn_gate_weight),
        "guT": by_rows(L0_ffn_gate_up_weights),
        "dnT": np.swapaxes(np.asarray(L0_ffn_down_weights), 1, 2),
        "sguT": by_rows(L0_ffn_shared_gate_up),
        "sdnT": np.asarray(L0_ffn_shared_down).T,
    }
    arrays = {n: np.ascontiguousarray(a) for n, a in arrays.items()}
    nc = bacc.Bacc("TRN2", target_bir_lowering=False, num_devices=1, dynamic_dma_scratch_size=8192)
    args = [nc.dram_tensor(n, a.shape, F32, kind="ExternalInput").ap() for n, a in arrays.items()]
    out = nc.dram_tensor("out", x.shape, F32, kind="ExternalOutput").ap()
    build(nc, *args, out)
    result = run_bass_kernel_spmd(nc, [arrays], core_ids=[0])
    return result.results[0]["out"]
```

```python
import numpy as np
import concourse.bass as bass
from concourse import mybir
from concourse.alu_op_type import AluOpType as ALU

ACT = mybir.ActivationFunctionType
F32 = mybir.dt.float32
U32 = mybir.dt.uint32
I32 = mybir.dt.int32
F32R = mybir.dt.float32r
AX = mybir.AxisListType

P = 128
LN_EPS = 1e-5
MASKED = -3.0e38


class SbufMap:

    def __init__(self, nc):
        self.nc = nc
        self.at = -(-nc.sbuf_base // 32) * 32

    def region(self, nbytes):
        start, self.at = self.at, self.at + -(-nbytes // 32) * 32
        assert self.at <= self.nc.sbuf_usable_end, self.at
        return start

    def tensor(self, name, shape, dtype=F32):
        return self.inside([self.region(4 * int(np.prod(shape[1:]))), None], name, shape, dtype)

    def inside(self, cursor, name, shape, dtype=F32):
        nbytes = -(-4 * int(np.prod(shape[1:])) // 32) * 32
        t = self.nc.alloc_sbuf_tensor_at(name, shape, dtype, offset=cursor[0])
        cursor[0] += nbytes
        assert cursor[1] is None or cursor[0] <= cursor[1], name
        return t


def build(nc, x, ctxT, wqT, wkvT, woT, gateT, guT, dnT, sguT, sdnT, out):
    NB, SQ, H = x.shape
    L = ctxT.shape[0]
    C = H // P
    HD = 32
    NH = H // HD
    R = P // HD
    E = guT.shape[0]
    F = dnT.shape[1]
    FS = sdnT.shape[0]
    T = NB * SQ
    TOPK = 2
    NT = (TOPK * T + E * (P - 1)) // P
    FK = [(k, min(P, F - k)) for k in range(0, F, P)]
    FSK = [(k, min(P, FS - k)) for k in range(0, FS, P)]
    NJ = len(FSK)
    SCALE = float(np.float32(1.0) / np.sqrt(np.float32(HD)))
    assert L == P and NT == 21 and NB == 8 and R == 4

    m = SbufMap(nc)
    GU, DN = C * 2 * F, len(FK) * H
    w_exp_at = m.region(4 * E * (GU + DN))
    w_gu = nc.alloc_sbuf_tensor_at("w_gu", [P, E * GU], F32, offset=w_exp_at)
    w_dn = nc.alloc_sbuf_tensor_at("w_dn", [P, E * DN], F32, offset=w_exp_at + 4 * E * GU)
    shared_at = m.region(4 * 2 * (C * 2 * F + len(FK) * H))
    shared_end = m.at
    xres = m.tensor("xres", [SQ, NB, H])
    x2T_at = m.region(4 * C * T)
    ident = m.tensor("ident", [P, P])
    small = [m.at, nc.sbuf_usable_end]

    def loaded_and_split(cursor, name, shape):
        at = cursor[0]
        raw = m.inside(cursor, name, shape)
        lo = nc.alloc_sbuf_tensor_at(name + "_lo", shape, F32R, offset=at)
        return raw, (m.inside(cursor, name + "_hi", shape, F32R), lo)

    w_gate, w_gate2 = loaded_and_split(small, "w_gate", [P, C, E])

    BLK = 4
    NBLK = NB // BLK
    W = BLK * SQ
    sh = [shared_at, shared_end]
    w_sg, w_sg2 = zip(*(loaded_and_split(sh, f"w_sg{i}", [P, C, 2 * P]) for i in range(2)))
    sg_end = sh[0]
    act_at = shared_end - 2 * 4 * 2 * H - 3 * 4 * W
    act_s, act_s2, silu_s = [None] * NBLK, [None] * NBLK, [None] * NBLK
    act0_at = small[0]
    for t, cursor in enumerate((small, [act_at, shared_end])):
        act_s[t], act_s2[t] = loaded_and_split(cursor, f"act_s{t}", [P, W])
        silu_s[t] = m.inside(cursor, f"silu_s{t}", [P, W])
    sh = [shared_end - 2 * 4 * 2 * H, shared_end]
    w_sd, w_sd2 = zip(*(loaded_and_split(sh, f"w_sd{i}", [P, H]) for i in range(2)))
    lgT = m.inside(small, "lgT", [E, T])

    att = [w_exp_at, shared_at]
    wq_at = att[1] - 2 * 4 * C * H
    w_q, w_q2 = loaded_and_split([wq_at, att[1]], "w_q", [P, C, H])
    w_kv, w_kv2 = loaded_and_split(att, "w_kv", [P, 2 * H])
    w_o, w_o2 = loaded_and_split(att, "w_o", [P, C, H])
    ctx, ctx2 = loaded_and_split(att, "ctx", [P, NB, SQ])
    mask = m.inside(att, "mask", [SQ, C, SQ])
    xn = [m.inside(att, f"xn{i}", [SQ, H]) for i in range(2)]
    xnT = []
    for k, cursor in enumerate((att, [x2T_at, x2T_at + 4 * C * T])):
        xnT.append(tuple(m.inside(cursor, f"xnT{k}_{part}", [P, C, W], F32R) for part in ("hi", "lo")))
    qT = [m.inside(att, f"qT{i}", [P, C, W]) for i in range(NBLK)]
    kT = [m.inside(att, f"kT{i}", [P, C, W]) for i in range(NBLK)]
    v_sb = m.inside(att, "v_sb", [SQ, H])
    score_at = [sg_end, shared_end - 2 * 4 * 2 * H]
    score = [m.inside(score_at, f"score{r}", [SQ, C, SQ]) for r in range(R)]
    prob = [m.inside(att, f"prob{r}", [SQ, C, SQ]) for r in range(R)]
    probT = [m.inside(att, f"probT{r}", [SQ, C, SQ]) for r in range(R)]
    oT = tuple(nc.alloc_sbuf_tensor_at(f"oT_{part}", [P, C, SQ], F32R, offset=at)
               for part, at in (("hi", act0_at), ("lo", act0_at + 4 * W)))
    x2T = (nc.alloc_sbuf_tensor_at("x2T_hi", [P, C, T], F32R, offset=x2T_at),
           nc.alloc_sbuf_tensor_at("x2T_lo", [P, C, T], F32R, offset=wq_at))
    keep = [att[0], wq_at]
    keep_from = keep[0]
    x2n = m.inside(keep, "x2n", [SQ, NB, H])
    dn_end = [w_exp_at + 4 * (E * GU + (e + 1) * DN) for e in range(E)]
    n_early = sum(end <= keep_from for end in dn_end)
    n_late = sum(end > wq_at for end in dn_end)
    loop = [x2T_at, x2T_at + 4 * C * T]
    pair = lambda cursor, name, shape: tuple(m.inside(cursor, f"{name}_{part}", shape, F32R) for part in ("hi", "lo"))
    xsT = pair(loop, "xsT", [P, C, P])
    silu_e = m.inside(loop, "silu_e", [P, F])
    act_e = m.inside(loop, "act_e", [P, len(FK) * P])
    actT_e = pair(loop, "actT_e", [P, len(FK), P])
    y_sb = m.inside(loop, "y_sb", [P, H])
    parts = [shared_at, shared_end]
    gu2 = pair(parts, "gu", [P, C, 2 * F])
    dn2 = pair(parts, "dn", [P, len(FK), H])
    gath = [shared_at, shared_end]
    y_tok = m.inside(gath, "y_tok", [SQ, NB, TOPK, H])

    sb = lambda name, shape, dtype=F32: m.inside(small, name, shape, dtype)
    xs_in = sb("xs_in", [P, H])
    zeros = xs_in
    negmax = sb("negmax", [SQ, R, C])
    rowsum = sb("rowsum", [SQ, R, C])
    rrow = sb("rrow", [SQ, R, C])
    bn1, mv1, var1, rstd1 = (sb(n, [SQ, NB, k]) for n, k in (("bn1", 6), ("mv1", 2), ("var1", 1), ("rstd1", 1)))
    bn2, mv2, var2, rstd2 = (sb(n, [SQ, NB, k]) for n, k in (("bn2", 6), ("mv2", 2), ("var2", 1), ("rstd2", 1)))
    minus_half = sb("minus_half", [SQ, 1])
    sb = lambda name, shape, dtype=F32: m.inside(keep, name, shape, dtype)
    tri = sb("tri", [SQ, SQ])
    ones = sb("ones", [SQ, P])
    down8 = sb("down8", [SQ, NB, E])
    below = sb("below", [P, E, E])
    thresh = sb("thresh", [P, E, T // P])
    tile_no = sb("tile_no", [1, NT, E])
    rt = lambda name: sb(name, [SQ, NB, E])
    logit, pexp, prb, eq, cand, oh1, oh2, prb2 = (rt(n) for n in "logit pexp prb eq cand oh1 oh2 prb2".split())
    rv = lambda name: sb(name, [SQ, NB])
    lmax, lsum, lrec, first1, first2 = (rv(n) for n in "lmax lsum lrec first1 first2".split())
    topw = m.inside(small, "topw", [SQ, TOPK, NB])
    picked = sb("picked", [SQ, NB + 1, E])
    before = sb("before", [SQ, NB + 1, E])
    count = sb("count", [P, E])
    overs = sb("over", [P, E, T // P])
    tiles = sb("tiles", [P, E])
    tilesb = sb("tilesb", [P, E, E])
    base = sb("base", [P, E])
    rank = rt("rank")
    slot = rt("slot")
    slot1 = rt("slot1")
    slot2 = rt("slot2")
    slot_i = m.inside(small, "slot_i", [SQ, TOPK, NB], U32)
    started = sb("started", [1, NT, E])
    eid_f = sb("eid_f", [1, NT])
    pair_f = sb("pair_f", [1, NT - 1])
    eid = m.inside(small, "eid", [1, NT], I32)
    eid2 = m.inside(small, "eid2", [1, NT - 1], I32)

    bank = [nc.alloc_psum_tensor(f"bank{i}", [P, 512], F32) for i in range(8)]
    S = bank[0:4]
    A, B, CC, D = bank[4:8]

    xs_dram = nc.dram_tensor("xs_dram", [NT * P, H], F32, kind="Internal")
    ys_dram = nc.dram_tensor("ys_dram", [NT * P, H], F32, kind="Internal")

    names = (
        "x0 x0b xrest wq wkv wo wgate ctx0 ctx1 wsg0 wsg1 wsd0 wsd1 we we_late "
        "const zt sel zero "
        "ctx_hi ctx_lo wkv_hi wkv_lo wq_hi wq_lo wq_lo2 wo_hi wo_lo wg_hi wg_lo wsg_hi wsg_lo wsd_hi wsd_lo "
        "bs1 st1 rs1a rs1b xn T1 xnT_hi xnT_lo Q QT K KT V Vs "
        "S ms mask exp rr prob prob3 PT probT O oT_hi oT_lo "
        "op x1 bs2 st2 rs2a rs2b x2n T2 x2T_hi x2T_lo "
        "lgT lgs lg rt rtc lexp trip rank rk pos scat "
        "sg ssil sact sact_hi sact_lo sdn sres "
        "pad pad_act xin Tx xs_hi xs_lo gu_hi gu_lo dn_hi dn_hi2 dn_lo dn_lo2 eg esil eact Ta aT_hi aT_lo edn ey yst fin out").split()
    s = {n: nc.alloc_semaphore(f"s_{n}") for n in names}
    s_gat = [nc.alloc_semaphore(f"s_gat{b}") for b in range(NB)]

    def chunked(b, n=H):
        return b[0:SQ, 0:n]

    def wait_alone(eng, sem, value):
        eng.wait_ge(sem, value)
        eng.nop(nofuse=True)

    with nc.Block() as block:

        @block.sync
        def _(sp):
            def load_ctx(k):
                at = slice(k * BLK, (k + 1) * BLK)
                sp.dma_start(ctx[:, at, :], ctxT[:, at, 0:SQ]).then_inc(s[f"ctx{k}"], 16)

            load_ctx(0)
            sp.dma_start(xres[:, 0, :], x[0]).then_inc(s["x0"], 16)
            sp.dma_start(w_kv[:, :], wkvT).then_inc(s["wkv"], 16)
            sp.dma_start(xres[:, 1:BLK, :], x[1:BLK].rearrange("b q d -> q b d")).then_inc(s["x0b"], 16)
            sp.dma_start(w_q[:, :, :], wqT.rearrange("(c p) d -> p c d", p=P)).then_inc(s["wq"], 16)
            sp.dma_start(xres[:, BLK:NB, :], x[BLK:NB].rearrange("b q d -> q b d")).then_inc(s["xrest"], 16)
            load_ctx(1)
            sp.dma_start(w_o[:, :, :], woT.rearrange("(c p) d -> p c d", p=P)).then_inc(s["wo"], 16)
            sp.dma_start(w_gate[:, :, :], gateT).then_inc(s["wgate"], 16)

            def load_sg(j):
                k, w = FSK[j]
                for n in range(2):
                    sp.dma_start(w_sg[j % 2][:, :, n * w:(n + 1) * w], sguT[:, :, n * FS + k:n * FS + k + w])\
                        .then_inc(s[f"wsg{j % 2}"], 16)

            def load_sd(j):
                k, w = FSK[j]
                sp.dma_start(w_sd[j % 2][0:w, :], sdnT[k:k + w, :]).then_inc(s[f"wsd{j % 2}"], 16)

            for j in range(2):
                load_sg(j)
                load_sd(j)
            sp.wait_ge(s["zt"], 1)
            sp.dma_start(xs_dram[:, :].rearrange("(n p) d -> p n d", p=P),
                         zeros[:, :].unsqueeze(1).to_broadcast([P, NT, H])).then_inc(s["zero"], 16)

            def load_gu(e, sem):
                sp.dma_start(w_gu[:, e * GU:(e + 1) * GU], guT[e].rearrange("p c f -> p (c f)")).then_inc(sem, 16)

            def load_dn(e, sem):
                k2 = F // P * P
                at = w_dn[:, e * DN:(e + 1) * DN].rearrange("p (k d) -> p k d", d=H)
                sp.dma_start(at[:, 0:k2 // P, :],
                             dnT[e, 0:k2, :].rearrange("(k p) d -> p k d", p=P)).then_inc(sem, 16)
                sp.dma_start(at[0:F - k2, k2 // P, :], dnT[e, k2:F, :]).then_inc(sem, 16)

            sp.wait_ge(s["op"], NB)

            def next_sg(j):
                sp.wait_ge(s["sg"], NBLK * (j - 1))
                load_sg(j)

            def next_sd(j):
                sp.wait_ge(s["sdn"], NB * (j - 1))
                load_sd(j)

            def load_x(i):
                sp.dma_start(xs_in[:, :], xs_dram[bass.ds(i * P, P), :]).then_inc(s["xin"], 16)

            for e in range(0, 2):
                load_gu(e, s["we"])
            next_sg(2)
            for e in range(2, 5):
                load_gu(e, s["we"])
            next_sg(3)
            next_sd(2)
            for e in range(5, E):
                load_gu(e, s["we"])
            for e in range(n_early):
                load_dn(e, s["we"])
            next_sg(4)
            next_sd(3)
            next_sg(5)
            next_sd(4)
            sp.wait_ge(s["pos"], 4)
            sp.wait_ge(s["scat"], 16 * TOPK * NB)
            load_x(0)
            for e in range(n_early, E - n_late):
                load_dn(e, s["we"])
            next_sd(5)
            sp.wait_ge(s["sg"], NBLK * NJ)
            for e in range(E - n_late, E):
                load_dn(e, s["we_late"])

            def store_y(i):
                sp.dma_start(ys_dram[bass.ds(i * P, P), :], y_sb[:, :]).then_inc(s["yst"], 16)

            for i in (1, 2):
                sp.wait_ge(s["Tx"], i)
                load_x(i)
            with sp.Fori(3, NT) as i:
                sp.wait_ge(s["Tx"], i)
                load_x(i)
                sp.wait_ge(s["ey"], i - 2)
                store_y(i - 3)
            for i in range(NT - 3, NT):
                sp.wait_ge(s["ey"], i + 1)
                store_y(i)
            for b in range(NB):
                sp.wait_ge(s["fin"], b + 1)
                sp.dma_start(out[b], xres[:, b, :]).then_inc(s["out"], 16)
            sp.wait_ge(s["out"], 16 * NB)

        @block.gpsimd
        def _(pool):
            cnt = [0]

            def own(ins):
                cnt[0] += 1
                ins.then_inc(s["sel"], 1)
                pool.wait_ge(s["sel"], cnt[0])

            own(pool.memset(ident[:, :], 0.0))
            pool.affine_select(out=ident[:, :], in_=ident[:, :], compare_op=ALU.not_equal, fill=1.0, base=0,
                               pattern=[[-1, P]], channel_multiplier=1).then_inc(s["const"], 1)
            pool.memset(minus_half[:, :], -0.5).then_inc(s["const"], 1)
            pool.memset(zeros[:, :], 0.0).then_inc(s["zt"], 1)
            own(pool.memset(mask[:, :, :], 0.0))
            pool.affine_select(out=mask[:, :, :], in_=mask[:, :, :], compare_op=ALU.is_ge, fill=MASKED, base=0,
                               pattern=[[0, C], [-1, SQ]], channel_multiplier=1).then_inc(s["const"], 1)
            pool.wait_ge(s["const"], 3)

            def normalised(b):
                r = R - 1
                pool.wait_ge(s["rr"], R * (b + 1))
                pool.tensor_tensor(prob[r][:, :, :], prob[r][:, :, :],
                                   rrow[:, r, :].unsqueeze(2).to_broadcast([SQ, C, SQ]), ALU.mult)\
                    .then_inc(s["prob3"], 1)

            def rstd(n, stats, var, rs, mv, own_sem, done):
                pool.wait_ge(s[stats], n + 1)
                pool.tensor_scalar(var[:, n, :], mv[:, n, 1:2], LN_EPS, 1.0, ALU.add, ALU.mult).then_inc(s[own_sem], 1)
                pool.wait_ge(s[own_sem], n + 1)
                pool.tensor_tensor(rs[:, n, :], var[:, n, :], minus_half[:, :], ALU.pow).then_inc(s[done], 1)

            for n in range(BLK):
                rstd(n, "st1", var1, rstd1, mv1, "rs1a", "rs1b")
            pool.wait_ge(s["wq_hi"], 1)
            half = slice(C // 2, C)
            pool.tensor_tensor(w_q2[1][:, half, :], w_q[:, half, :], w_q2[0][:, half, :].bitcast(F32), ALU.subtract)\
                .then_inc(s["wq_lo2"], 1)
            for n in range(BLK, NB):
                rstd(n, "st1", var1, rstd1, mv1, "rs1a", "rs1b")
            pool.wait_ge(s["wo"], 16)
            pool.tensor_copy(w_o2[0][:, :, :], w_o[:, :, :]).then_inc(s["wo_hi"], 1)
            pool.wait_ge(s["wo_hi"], 1)
            pool.tensor_tensor(w_o2[1][:, :, :], w_o[:, :, :], w_o2[0][:, :, :].bitcast(F32), ALU.subtract)\
                .then_inc(s["wo_lo"], 1)
            own(pool.memset(tri[:, :], 1.0))
            own(pool.affine_select(out=tri[:, :], in_=tri[:, :], compare_op=ALU.is_gt, fill=0.0, base=0,
                                   pattern=[[1, SQ]], channel_multiplier=-1))
            own(pool.memset(ones[:, :], 1.0))
            own(pool.iota(down8[:, :, :], [[0, NB], [-1, E]], base=E, channel_multiplier=0,
                          allow_small_or_imprecise_dtypes=True))
            own(pool.memset(below[:, :, :], 1.0))
            own(pool.affine_select(out=below[:, :, :], in_=below[:, :, :], compare_op=ALU.is_gt, fill=0.0, base=0,
                                   pattern=[[1, E], [-1, E]], channel_multiplier=0))
            own(pool.iota(thresh[:, :, :], [[0, E], [P, T // P]], base=0, channel_multiplier=0,
                          allow_small_or_imprecise_dtypes=True))
            own(pool.iota(tile_no[:, :, :], [[1, NT], [0, E]], base=0, channel_multiplier=0,
                          allow_small_or_imprecise_dtypes=True))
            pool.memset(before[:, 0:1, :], 0.0).then_inc(s["const"], 1)
            normalised(0)
            for n in range(1, NB):
                if n >= 2:
                    rstd(n - 2, "st2", var2, rstd2, mv2, "rs2a", "rs2b")
                normalised(n)
            for n in (NB - 2, NB - 1):
                rstd(n, "st2", var2, rstd2, mv2, "rs2a", "rs2b")

            pool.wait_ge(s["zero"], 16)
            pool.wait_ge(s["x2n"], NB)
            pool.wait_ge(s["pos"], 2)
            for b in range(NB):
                for k in range(TOPK):
                    pool.indirect_dma_start(
                        out=xs_dram[:, :], out_offset=bass.IndirectOffsetOnAxis(ap=slot_i[:, k, b:b + 1], axis=0),
                        in_=x2n[:, b, :], in_offset=None).then_inc(s["scat"], 16)
            def dn_parts(i, first=False):
                e = pool.value_load(eid[0:1, bass.ds(i, 1)], min_val=0, max_val=E - 1)
                w = FK[-1][1]
                last = w_dn[0:w, bass.ds(e * DN + 2 * H, H)]
                if not first:
                    pool.wait_ge(s["edn"], len(FK) * i)
                pool.tensor_copy(dn2[0][0:w, 2, :], last).then_inc(s["dn_hi2"], 1)
                wait_alone(pool, s["dn_hi2"], i + 1)
                pool.tensor_tensor(dn2[1][0:w, 2, :], last, dn2[0][0:w, 2, :].bitcast(F32), ALU.subtract)\
                    .then_inc(s["dn_lo2"], 1)
                wait_alone(pool, s["dn_hi"], 2 * (i + 1))
                pool.tensor_tensor(dn2[1][:, 1, :], w_dn[:, bass.ds(e * DN + H, H)], dn2[0][:, 1, :].bitcast(F32),
                                   ALU.subtract).then_inc(s["dn_lo2"], 1)

            assert len(FK) == 3
            pool.wait_ge(s["pos"], 4)
            pool.wait_ge(s["we"], 16 * (3 * E - 2 * n_late))
            pool.wait_ge(s["we_late"], 16 * 2 * n_late)
            pool.wait_ge(s["sdn"], NB * NJ)
            rest = FK[-1][1]
            for t in (dn2[0], dn2[1]):
                pool.memset(t[rest:P, len(FK) - 1, :].bitcast(F32), 0.0).then_inc(s["pad"], 1)
            pool.wait_ge(s["pad"], 2)
            dn_parts(0, first=True)
            with pool.Fori(1, NT) as i:
                dn_parts(i)
            pool.wait_ge(s["yst"], 16 * NT)
            for b in range(NB):
                for k in range(TOPK):
                    pool.indirect_dma_start(
                        out=y_tok[:, b, k, :], out_offset=None, in_=ys_dram[:, :],
                        in_offset=bass.IndirectOffsetOnAxis(ap=slot_i[:, k, b:b + 1], axis=0)).then_inc(s_gat[b], 16)

        @block.tensor
        def _(pe):
            def transposes(dst, src):
                for c in range(C):
                    ins = pe.transpose(dst[:, c * SQ:(c + 1) * SQ], src[:, c * P:(c + 1) * P], ident[0:SQ, 0:SQ])
                return ins

            def product(dst, terms, start=True, stop=True, first=0, last=None):
                passes = [(a[i], b[j]) for a, b in terms for i, j in ((1, 0), (0, 1), (0, 0))]
                for n, (a, b) in list(enumerate(passes))[first:last]:
                    ins = pe.matmul(dst, a, b, start=start and n == 0, stop=stop and n == len(passes) - 1)
                return ins

            def both(pair, *at):
                return tuple(t[at] for t in pair)

            every = slice(None)

            def t1(n, bank_):
                pe.wait_ge(s["xn"], n + 1)
                transposes(bank_, xn[n % 2]).then_inc(s["T1"], 1)

            def q_proj(k, j, bank_):
                product(bank_[:, 0:W], [(both(w_q2, every, c, slice(j * P, (j + 1) * P)), both(xnT[k], every, c, every))
                                        for c in range(C)]).then_inc(s["Q"], 1)

            def k_proj(k, j, bank_):
                product(bank_[:, 0:W], [(both(w_kv2, every, slice(j * P, (j + 1) * P)),
                                         both(ctx2, every, slice(k * BLK, (k + 1) * BLK), every))]).then_inc(s["K"], 1)

            def v_proj(n):
                product(A[0:SQ, :], [(both(ctx2, every, n, every), both(w_kv2, every, slice(H, 2 * H)))])\
                    .then_inc(s["V"], 1)

            def out_proj(n, first, last):
                pe.wait_ge(s["oT_hi"], n + 1)
                pe.wait_ge(s["oT_lo"], n + 1)
                ins = product(D[0:SQ, :], [(both(oT, every, c, every), both(w_o2, every, c, every))
                                           for c in range(C)], first=first, last=last)
                if last == 3 * C:
                    ins.then_inc(s["op"], 1)

            def t2(n):
                pe.wait_ge(s["x2n"], n + 1)
                for c in range(C):
                    ins = pe.transpose(B[:, c * SQ:(c + 1) * SQ], x2n[:, n, c * P:(c + 1) * P], ident[0:SQ, 0:SQ])
                ins.then_inc(s["T2"], 1)

            def scores(b):
                k, cols = b // BLK, slice(b % BLK * SQ, (b % BLK + 1) * SQ)
                pe.wait_ge(s["QT"], C * (k + 1))
                pe.wait_ge(s["KT"], C * (k + 1))
                for c in range(C):
                    for r in range(R):
                        rows = slice(HD * r, HD * (r + 1))
                        ins = pe.matmul(S[r][0:SQ, c * SQ:(c + 1) * SQ], qT[k][rows, c, cols], kT[k][rows, c, cols],
                                        start=True, stop=True)
                        if c == C - 1:
                            ins.then_inc(s["S"], 1)

            def shared_gu(j, t, halves=(0, 1)):
                k, w = FSK[j]
                n = NBLK * j + t
                dst = (S[2 * t], S[2 * t + 1])
                if t == 0 and halves[0] == 0:
                    pe.wait_ge(s["wsg_hi"], j + 1)
                    pe.wait_ge(s["wsg_lo"], j + 1)
                if j >= 1:
                    pe.wait_ge(s["sact"], n - NBLK + 1)
                cols = slice(t * W, (t + 1) * W)
                for h in halves[0:-(-2 * w // P)]:
                    ins = product(dst[h][:, 0:W], [(both(w_sg2[j % 2], every, c, slice(h * P, (h + 1) * P)),
                                                    both(x2T, every, c, cols)) for c in range(C)])
                if halves[-1] == 1:
                    ins.then_inc(s["sg"], 1)

            pe.wait_ge(s["const"], 1)
            t1(0, S[0])
            for what in ("ctx_hi", "ctx_lo", "wkv_hi", "wkv_lo"):
                pe.wait_ge(s[what], 1)
            k_proj(0, 0, bank[4])
            for j in range(1, C):
                k_proj(0, j, bank[4 + j])
                t1(j, S[j])
            for what, value in (("wq_hi", 1), ("wq_lo", 1), ("wq_lo2", 1), ("xnT_hi", BLK), ("xnT_lo", BLK)):
                pe.wait_ge(s[what], value)
            for j in range(C):
                pe.wait_ge(s["KT"], j + 1)
                q_proj(0, j, bank[4 + j])
                t1(BLK + j, S[j])
            pe.wait_ge(s["xnT_hi"], NB)
            pe.wait_ge(s["xnT_lo"], NB)
            scores(0)
            v_proj(0)
            pe.wait_ge(s["ctx_hi"], 2)
            pe.wait_ge(s["ctx_lo"], 2)

            def fill(j):
                q_proj(1, j, D)
                k_proj(1, j, CC)

            fill(0)
            for b in range(NB):
                if b + 1 < NB:
                    pe.wait_ge(s["mask"], R * (b + 1))
                    scores(b + 1)
                else:
                    pe.wait_ge(s["mask"], R * NB)
                    pe.wait_ge(s["x2T_hi"], BLK)
                    pe.wait_ge(s["x2T_lo"], BLK)
                    shared_gu(0, 0, (0,))
                if 1 <= b + 1 < C:
                    pe.wait_ge(s["QT"], C + b + 1)
                    if b >= 2:
                        pe.wait_ge(s["x1"], b - 1)
                    pe.wait_ge(s["KT"], C + b + 1)
                    if b >= 1:
                        pe.wait_ge(s["oT_hi"], b)
                        pe.wait_ge(s["oT_lo"], b)
                    fill(b + 1)
                if b >= 2:
                    t2(b - 2)
                for r in range(R):
                    if r == 1 and b >= 1:
                        pe.wait_ge(s["QT"], C * NBLK if b >= C - 1 else C + b + 2)
                        if b >= 2:
                            pe.wait_ge(s["x1"], b - 1)
                        if b == 1:
                            pe.wait_ge(s["wo_hi"], 1)
                            pe.wait_ge(s["wo_lo"], 1)
                        out_proj(b - 1, 0, 7)
                    if r == 3 and b >= 1:
                        out_proj(b - 1, 7, 9)
                    if r < R - 1:
                        pe.wait_ge(s["prob"], (R - 1) * b + r + 1)
                    else:
                        pe.wait_ge(s["prob3"], b + 1)
                    if r == 0:
                        pe.wait_ge(s["Vs"], b + 1)
                    if r == 1 and b >= 2:
                        pe.wait_ge(s["x2T_hi"], b - 1)
                        pe.wait_ge(s["x2T_lo"], b - 1)
                    if r >= 2:
                        pe.wait_ge(s["probT"], R * b + r - 1)
                    for c in range(C):
                        ins = pe.transpose((A, B)[r % 2][0:SQ, c * SQ:(c + 1) * SQ], prob[r][:, c, :],
                                           ident[0:SQ, 0:SQ])
                    ins.then_inc(s["PT"], 1)
                if b >= 1:
                    out_proj(b - 1, 9, 3 * C)
                pe.wait_ge(s["KT"], C * NBLK if b >= C - 1 else C + b + 2)
                for h in range(NH):
                    r, c = h % R, h // R
                    if c == 0:
                        pe.wait_ge(s["probT"], R * b + r + 1)
                    ins = pe.matmul(CC[HD * r:HD * (r + 1), c * SQ:(c + 1) * SQ], v_sb[:, h * HD:(h + 1) * HD],
                                    probT[r][:, c, :], start=True, stop=True)
                ins.then_inc(s["O"], 1)
                if b + 1 < NB:
                    v_proj(b + 1)
            shared_gu(0, 0, (1,))
            t2(NB - 2)
            pe.wait_ge(s["x1"], NB - 1)
            out_proj(NB - 1, 0, 3 * C)

            def t_x(i):
                pe.wait_ge(s["xin"], 16 * i + 16)
                for c in range(C):
                    ins = pe.transpose(S[2][:, c * P:(c + 1) * P], xs_in[:, c * P:(c + 1) * P], ident[:, :])
                ins.then_inc(s["Tx"], 1)

            out_bank = (B, CC, D, A)

            def shared_down(j, t):
                k, w = FSK[j]
                pe.wait_ge(s["wsd_hi"], j + 1)
                pe.wait_ge(s["wsd_lo"], j + 1)
                pe.wait_ge(s["sact_hi"], NBLK * j + t + 1)
                pe.wait_ge(s["sact_lo"], NBLK * j + t + 1)
                for i in range(BLK):
                    n = NB * j + t * BLK + i
                    if n >= BLK:
                        pe.wait_ge(s["sres"], n - BLK + 1)
                    if n == BLK - 1:
                        pe.wait_ge(s["rt"], 1)
                    if n == NB + BLK - 1:
                        pe.wait_ge(s["rk"], 2)
                    product(out_bank[i][0:SQ, :], [(both(act_s2[t], slice(0, w), slice(i * SQ, (i + 1) * SQ)),
                                                    both(w_sd2[j % 2], slice(0, w), every))]).then_inc(s["sdn"], 1)

            def logits(t):
                product((CC, D)[t][0:E, 0:W], [(both(w_gate2, every, c, every), both(x2T, every, c, slice(t * W, (t + 1) * W)))
                                               for c in range(C)]).then_inc(s["lgT"], 1)

            pe.wait_ge(s["oT_lo"], NB)
            pe.wait_ge(s["wg_hi"], 1)
            pe.wait_ge(s["wg_lo"], 1)
            logits(0)
            pe.wait_ge(s["x2T_hi"], NB - 1)
            pe.wait_ge(s["x2T_lo"], NB - 1)
            t2(NB - 1)
            shared_gu(1, 0, (0,))
            pe.wait_ge(s["x2T_hi"], NB)
            pe.wait_ge(s["x2T_lo"], NB)
            shared_gu(0, 1)
            pe.wait_ge(s["x1"], NB)
            logits(1)
            shared_gu(1, 0, (1,))
            pe.wait_ge(s["lgs"], NBLK)
            for b in range(NB):
                ins = pe.transpose(A[0:SQ, b * E:(b + 1) * E], lgT[:, b * SQ:(b + 1) * SQ], ident[0:E, 0:E])
            ins.then_inc(s["lg"], 1)
            shared_down(0, 0)
            shared_gu(1, 1)
            shared_down(0, 1)
            shared_gu(2, 0)
            pe.wait_ge(s["trip"], 1)
            pe.wait_ge(s["sres"], NB)
            pe.matmul(A[0:SQ, 0:NB * E], tri[:, :], picked[:, 0:NB, :], start=True, stop=False)
            pe.matmul(A[0:SQ, 0:NB * E], ones[:, 0:SQ], before[:, 0:NB, :], start=False, stop=True).then_inc(s["rank"], 1)
            pe.matmul(A[:, NB * E:(NB + 1) * E], ones[:, :], before[:, NB, :], start=True, stop=True)\
                .then_inc(s["rank"], 1)
            shared_down(1, 0)
            shared_gu(2, 1)
            shared_down(1, 1)
            for j in range(3, NJ):
                shared_gu(j, 0)
                shared_down(j - 1, 0)
                shared_gu(j, 1)
                shared_down(j - 1, 1)
            shared_down(NJ - 1, 0)
            pe.wait_ge(s["sact"], NBLK * NJ)
            t_x(0)
            shared_down(NJ - 1, 1)

            def gate_up(i):
                pe.wait_ge(s["xs_hi"], i + 1)
                pe.wait_ge(s["xs_lo"], i + 1)
                for c in range(C):
                    pe.wait_ge(s["gu_hi"], C * i + c + 1)
                    pe.wait_ge(s["gu_lo"], C * i + c + 1)
                    for n, (x_, w_) in enumerate(((0, 1), (0, 0), (1, 0))):
                        for dst, f0 in ((S[0], 0), (S[1], F)):
                            ins = pe.matmul(dst[:, 0:F], xsT[x_][:, c, :], gu2[w_][:, c, f0:f0 + F],
                                            start=c == 0 and n == 0, stop=c == C - 1 and n == 2)
                    ins.then_inc(s["eg"], 1)

            def down(i):
                pe.wait_ge(s["aT_hi"], i + 1)
                pe.wait_ge(s["aT_lo"], i + 1)
                for j in range(len(FK)):
                    if j == 0:
                        pe.wait_ge(s["dn_hi"], 2 * (i + 1))
                        pe.wait_ge(s["dn_lo"], i + 1)
                    else:
                        pe.wait_ge(s["dn_lo2"], 2 * (i + 1))
                    product(A[:, :], [(both(actT_e, every, j, every), both(dn2, every, j, every))],
                            j == 0, j == len(FK) - 1).then_inc(s["edn"], 1)

            def t_act(i):
                pe.wait_ge(s["eact"], i + 1)
                for j in range(len(FK)):
                    ins = pe.transpose(S[3][:, j * P:(j + 1) * P], act_e[:, j * P:(j + 1) * P], ident[:, :])
                ins.then_inc(s["Ta"], 1)

            gate_up(0)
            t_x(1)
            pe.wait_ge(s["sres"], NB * NJ)
            pe.wait_ge(s["pad"], 2)
            pe.wait_ge(s["pad_act"], 1)
            t_act(0)
            gate_up(1)
            t_x(2)
            down(0)
            t_act(1)
            with pe.Fori(2, NT - 1) as i:
                gate_up(i)
                t_x(i + 1)
                pe.wait_ge(s["ey"], i - 1)
                down(i - 1)
                t_act(i)
            gate_up(NT - 1)
            pe.wait_ge(s["ey"], NT - 2)
            down(NT - 2)
            t_act(NT - 1)
            pe.wait_ge(s["ey"], NT - 1)
            down(NT - 1)

        @block.scalar
        def _(act):
            def copy_out(dst, src, sem):
                act.activation(dst, src, ACT.Copy).then_inc(s[sem], 1)

            def as_chunks(b, w=SQ, p=P):
                return b[0:p, 0:C * w].rearrange("p (c q) -> p c q", c=C)

            def hi(dst, src, sem):
                copy_out(dst, src, sem)

            def put_xnT(n, bank_):
                act.wait_ge(s["T1"], n + 1)
                at = n % BLK * SQ
                hi(xnT[n // BLK][0][:, :, at:at + SQ], as_chunks(bank_), "xnT_hi")

            def put_qT(k, j, bank_):
                act.wait_ge(s["Q"], C * k + j + 1)
                copy_out(qT[k][:, j, :], bank_[:, 0:W], "QT")

            def put_kT(k, j, bank_):
                act.wait_ge(s["K"], C * k + j + 1)
                copy_out(kT[k][:, j, :], bank_[:, 0:W], "KT")

            def put_v(n):
                act.wait_ge(s["V"], n + 1)
                copy_out(v_sb[:, :], A[0:SQ, :], "Vs")

            def put_x2T(n):
                act.wait_ge(s["T2"], n + 1)
                hi(x2T[0][:, :, n * SQ:(n + 1) * SQ], as_chunks(B), "x2T_hi")

            def sg_hi(j):
                act.wait_ge(s[f"wsg{j % 2}"], 32 * (j // 2 + 1))
                w2 = 2 * FSK[j][1]
                hi(w_sg2[j % 2][0][:, :, 0:w2], w_sg[j % 2][:, :, 0:w2], "wsg_hi")

            def sd_hi(j):
                act.wait_ge(s[f"wsd{j % 2}"], 16 * (j // 2 + 1))
                w = FSK[j][1]
                hi(w_sd2[j % 2][0][0:w, :], w_sd[j % 2][0:w, :], "wsd_hi")

            def exps(b, r):
                act.wait_ge(s["mask"], R * b + r + 1)
                if b >= 1:
                    act.wait_ge(s["PT"], R * (b - 1) + r + 1)
                for c in range(C):
                    ins = act.activation(prob[r][:, c, :], score[r][:, c, :], ACT.Exp, bias=negmax[:, r, c:c + 1],
                                         accum_out=rowsum[:, r, c:c + 1])
                ins.then_inc(s["exp"], 1)

            def put_pT(b, r):
                act.wait_ge(s["PT"], R * b + r + 1)
                copy_out(probT[r][:, :, :], as_chunks((A, B)[r % 2], p=SQ), "probT")

            def ctx_hi(k):
                act.wait_ge(s[f"ctx{k}"], 16)
                at = slice(k * BLK, (k + 1) * BLK)
                hi(ctx2[0][:, at, :], ctx[:, at, :], "ctx_hi")

            ctx_hi(0)
            act.wait_ge(s["wkv"], 16)
            hi(w_kv2[0][:, :], w_kv[:, :], "wkv_hi")
            put_xnT(0, S[0])
            put_kT(0, 0, bank[4])
            act.wait_ge(s["wq"], 16)
            hi(w_q2[0][:, :, :], w_q[:, :, :], "wq_hi")
            for j in range(1, C):
                put_kT(0, j, bank[4 + j])
                put_xnT(j, S[j])
            ctx_hi(1)
            for j in range(C):
                put_qT(0, j, bank[4 + j])
                put_xnT(BLK + j, S[j])
            for r in range(R):
                exps(0, r)
            put_v(0)
            put_qT(1, 0, D)
            put_kT(1, 0, CC)
            for b in range(NB):
                if 1 <= b + 1 < C:
                    put_qT(1, b + 1, D)
                    put_kT(1, b + 1, CC)
                if b >= 2:
                    put_x2T(b - 2)
                if b == 2:
                    act.wait_ge(s["wgate"], 16)
                    hi(w_gate2[0][:, :, :], w_gate[:, :, :], "wg_hi")
                put_pT(b, 0)
                if b + 1 < NB:
                    exps(b + 1, 0)
                for r in range(1, R):
                    put_pT(b, r)
                if b + 1 < NB:
                    exps(b + 1, 1)
                if b == NB - 1:
                    sg_hi(1)
                    sd_hi(1)
                act.wait_ge(s["O"], b + 1)
                hi(oT[0][:, :, :], as_chunks(CC), "oT_hi")
                if b + 1 < NB:
                    put_v(b + 1)
                    exps(b + 1, 2)
                    exps(b + 1, 3)
                if b == 0:
                    sg_hi(0)
                    sd_hi(0)

            def shared_silu(j, t):
                w = FSK[j][1]
                act.wait_ge(s["sg"], NBLK * j + t + 1)
                act.activation(silu_s[t][0:w, :], S[2 * t][0:w, 0:W], ACT.Silu).then_inc(s["ssil"], 1)

            def shared_hi(j, t):
                w = FSK[j][1]
                n = NBLK * j + t
                if j >= 1:
                    act.wait_ge(s["sdn"], NB * (j - 1) + BLK * (t + 1))
                act.wait_ge(s["sact"], n + 1)
                hi(act_s2[t][0][0:w, :], act_s[t][0:w, :], "sact_hi")

            def put_logits(t):
                act.wait_ge(s["lgT"], t + 1)
                copy_out(lgT[:, t * W:(t + 1) * W], (CC, D)[t][0:E, 0:W], "lgs")

            put_x2T(NB - 2)
            shared_silu(0, 0)
            shared_hi(0, 0)
            put_x2T(NB - 1)
            put_logits(0)
            shared_silu(0, 1)
            shared_hi(0, 1)
            put_logits(1)
            sg_hi(2)
            shared_silu(1, 0)
            act.wait_ge(s["rt"], 1)
            act.activation(pexp[:, :, :], logit[:, :, :], ACT.Exp).then_inc(s["lexp"], 1)
            shared_hi(1, 0)
            shared_silu(1, 1)
            shared_hi(1, 1)
            sg_hi(3)
            sd_hi(2)
            for j in range(2, NJ):
                shared_silu(j, 0)
                shared_hi(j, 0)
                shared_silu(j, 1)
                shared_hi(j, 1)
                if j + 2 < NJ:
                    sg_hi(j + 2)
                if j + 1 < NJ:
                    sd_hi(j + 1)

            def xs_hi(i):
                act.wait_ge(s["Tx"], i + 1)
                hi(xsT[0][:, :, :], as_chunks(S[2], w=P), "xs_hi")

            def expert(i):
                return act.value_load(eid[0:1, bass.ds(i, 1)], min_val=0, max_val=E - 1)

            def experts(i):
                both_ = act.value_load(eid2[0:1, bass.ds(i, 1)], min_val=0, max_val=E * E - 1)
                return both_ % E, both_ // E

            def gu_hi(e, i, c, first=False):
                if not first:
                    act.wait_ge(s["eg"], C * (i - 1) + c + 1)
                hi(gu2[0][:, c, :], w_gu[:, bass.ds(e * GU + c * 2 * F, 2 * F)], "gu_hi")

            def dn_hi(e, i, first=False):
                for j in range(2):
                    if not first:
                        act.wait_ge(s["edn"], len(FK) * (i - 1) + j + 1)
                    hi(dn2[0][:, j, :], w_dn[:, bass.ds(e * DN + j * H, H)], "dn_hi")

            def silu(i):
                act.wait_ge(s["eg"], C * (i + 1))
                act.activation(silu_e[:, :], S[0][:, 0:F], ACT.Silu).then_inc(s["esil"], 1)

            def put_y(i, wait=True):
                act.wait_ge(s["edn"], len(FK) * (i + 1))
                if wait:
                    act.wait_ge(s["yst"], 16 * i)
                copy_out(y_sb[:, :], A[:, :], "ey")

            def aT_hi(i):
                act.wait_ge(s["Ta"], i + 1)
                hi(actT_e[0][:, :, :], S[3][:, 0:len(FK) * P].rearrange("p (k t) -> p k t", t=P), "aT_hi")

            def step(i, first=False, second=False):
                e, e_next = experts(i)
                for c in range(C - 1):
                    gu_hi(e_next, i + 1, c)
                silu(i)
                xs_hi(i + 1)
                gu_hi(e_next, i + 1, C - 1)
                dn_hi(e, i, first=first)
                if not first:
                    put_y(i - 1, wait=not second)
                aT_hi(i)

            act.wait_ge(s["pos"], 4)
            act.wait_ge(s["we"], 16 * (3 * E - 2 * n_late))
            xs_hi(0)
            for c in range(C):
                gu_hi(expert(0), 0, c, first=True)
            act.wait_ge(s["sdn"], NB * NJ)
            act.wait_ge(s["we_late"], 16 * 2 * n_late)
            step(0, first=True)
            step(1, second=True)
            with act.Fori(2, NT - 1) as i:
                step(i)
            silu(NT - 1)
            dn_hi(expert(NT - 1), NT - 1)
            put_y(NT - 2)
            aT_hi(NT - 1)
            put_y(NT - 1)

        @block.vector
        def _(dve):
            def stats(n, bn, mv, own_sem, done):
                dve.bn_stats(bn[:, n, :], xres[:, n, :]).then_inc(s[own_sem], 1)
                dve.wait_ge(s[own_sem], n + 1)
                dve.bn_aggr(mv[:, n, :], bn[:, n, :]).then_inc(s[done], 1)

            def apply(n, dst, mv, rs, ready, done):
                dve.wait_ge(s[ready], n + 1)
                dve.tensor_scalar(dst, xres[:, n, :], mv[:, n, 0:1], rs[:, n, :],
                                  ALU.subtract, ALU.mult).then_inc(s[done], 1)

            def lo(parts, src, hi_sem, value, sem, at):
                dve.wait_ge(s[hi_sem], value)
                hi_, lo_ = (t[at] for t in parts)
                dve.tensor_tensor(lo_, src, hi_.bitcast(F32), ALU.subtract).then_inc(s[sem], 1)

            def as_chunks(b, w=SQ):
                return b[:, 0:C * w].rearrange("p (c q) -> p c q", c=C)

            def stats1(n):
                stats(n, bn1, mv1, "bs1", "st1")

            def apply1(n):
                if n >= 2:
                    dve.wait_ge(s["T1"], n - 1)
                apply(n, xn[n % 2][:, :], mv1, rstd1, "rs1b", "xn")

            def xnT_lo(n, bank_):
                at = n % BLK * SQ
                lo(xnT[n // BLK], as_chunks(bank_), "xnT_hi", n + 1, "xnT_lo", (slice(None), slice(None), slice(at, at + SQ)))

            def add_attention(n):
                dve.wait_ge(s["op"], n + 1)
                dve.tensor_tensor(xres[:, n, :], xres[:, n, :], D[0:SQ, :], ALU.add).then_inc(s["x1"], 1)
                dve.wait_ge(s["x1"], n + 1)
                stats(n, bn2, mv2, "bs2", "st2")

            def apply2(n):
                apply(n, x2n[:, n, :], mv2, rstd2, "rs2b", "x2n")

            def x2T_lo(n):
                lo(x2T, as_chunks(B), "x2T_hi", n + 1, "x2T_lo", (slice(None), slice(None), slice(n * SQ, (n + 1) * SQ)))

            def sg_lo(j):
                at = (slice(None), slice(None), slice(0, 2 * FSK[j][1]))
                lo(w_sg2[j % 2], w_sg[j % 2][at], "wsg_hi", j + 1, "wsg_lo", at)

            def sd_lo(j):
                at = (slice(0, FSK[j][1]), slice(None))
                lo(w_sd2[j % 2], w_sd[j % 2][at], "wsd_hi", j + 1, "wsd_lo", at)

            def masked(b, r):
                dve.wait_ge(s["S"], R * b + r + 1)
                dve.scalar_tensor_tensor(out=score[r][:, :, :].rearrange("p c k -> p (c k)"),
                                         in0=S[r][0:SQ, 0:C * SQ], scalar=SCALE,
                                         in1=mask[:, :, :].rearrange("p c k -> p (c k)"),
                                         op0=ALU.mult, op1=ALU.add).then_inc(s["ms"], 1)
                dve.wait_ge(s["ms"], R * b + r + 1)
                dve.tensor_reduce(negmax[:, r, :], score[r][:, :, :], AX.X, ALU.max, negate=True)\
                   .then_inc(s["mask"], 1)

            def normalised(b, r):
                dve.wait_ge(s["exp"], R * b + r + 1)
                dve.reciprocal(rrow[:, r, :], rowsum[:, r, :]).then_inc(s["rr"], 1)
                if r == R - 1:
                    return
                dve.wait_ge(s["rr"], R * b + r + 1)
                dve.tensor_tensor(prob[r][:, :, :], prob[r][:, :, :],
                                  rrow[:, r, :].unsqueeze(2).to_broadcast([SQ, C, SQ]), ALU.mult)\
                   .then_inc(s["prob"], 1)

            whole = slice(None)
            dve.wait_ge(s["x0"], 16)
            stats1(0)

            def ctx_lo(k):
                dve.wait_ge(s[f"ctx{k}"], 16)
                at = slice(k * BLK, (k + 1) * BLK)
                lo(ctx2, ctx[:, at, :], "ctx_hi", k + 1, "ctx_lo", (whole, at, whole))

            ctx_lo(0)
            apply1(0)
            dve.wait_ge(s["wkv"], 16)
            lo(w_kv2, w_kv[:, :], "wkv_hi", 1, "wkv_lo", (whole, whole))
            dve.wait_ge(s["x0b"], 16)
            stats1(1)
            stats1(2)
            apply1(1)
            xnT_lo(0, S[0])
            stats1(3)
            apply1(2)
            xnT_lo(1, S[1])
            apply1(3)
            dve.wait_ge(s["wq"], 16)
            half = slice(0, C // 2)
            lo(w_q2, w_q[:, half, :], "wq_hi", 1, "wq_lo", (whole, half, whole))
            for n in range(2, BLK):
                xnT_lo(n, S[n])
            ctx_lo(1)
            dve.wait_ge(s["xrest"], 16)
            stats1(BLK)
            for n in range(BLK, NB):
                if n + 1 < NB:
                    stats1(n + 1)
                apply1(n)
                if n > BLK:
                    xnT_lo(n - 1, S[n - 1 - BLK])
            xnT_lo(NB - 1, S[BLK - 1])
            dve.wait_ge(s["const"], 3)
            for r in range(R):
                masked(0, r)
            for r in range(R):
                normalised(0, r)
            for b in range(NB):
                for r in range(R):
                    if b + 1 < NB:
                        masked(b + 1, r)
                    if b >= 3 and r == 0 or b == 2 and r == 1:
                        x2T_lo(b - 2)
                if b == 2:
                    lo(w_gate2, w_gate[:, :, :], "wg_hi", 1, "wg_lo", (whole, whole, whole))
                if b >= 1:
                    add_attention(b - 1)
                if b + 1 < NB:
                    normalised(b + 1, 0)
                    normalised(b + 1, 1)
                if b >= 1:
                    apply2(b - 1)
                lo(oT, as_chunks(CC), "oT_hi", b + 1, "oT_lo", (whole, whole, whole))
                if b + 1 < NB:
                    normalised(b + 1, 2)
                    normalised(b + 1, 3)
                if b == 0:
                    sg_lo(0)
                    sd_lo(0)
                if b == NB - 1:
                    sg_lo(1)
                    sd_lo(1)
            add_attention(NB - 1)
            x2T_lo(NB - 2)
            apply2(NB - 1)

            def shared_act(j, t):
                k, w = FSK[j]
                n = NBLK * j + t
                dve.wait_ge(s["ssil"], n + 1)
                if j >= 1:
                    dve.wait_ge(s["sdn"], NB * (j - 1) + BLK * (t + 1))
                up = S[2 * t + 1][0:w, 0:W] if 2 * w > P else S[2 * t][w:2 * w, 0:W]
                dve.tensor_tensor(act_s[t][0:w, :], up, silu_s[t][0:w, :], ALU.mult).then_inc(s["sact"], 1)
                lo(act_s2[t], act_s[t][0:w, :], "sact_hi", n + 1, "sact_lo", (slice(0, w), whole))

            def add_shared(j, t):
                for i in range(BLK):
                    b = t * BLK + i
                    dve.wait_ge(s["sdn"], NB * j + b + 1)
                    dve.tensor_tensor(xres[:, b, :], xres[:, b, :], (B, CC, D, A)[i][0:SQ, :], ALU.add)\
                       .then_inc(s["sres"], 1)

            cnt = [0]

            def link(ins):
                cnt[0] += 1
                ins.then_inc(s["rtc"], 1)
                dve.wait_ge(s["rtc"], cnt[0])

            def over_e(v):
                return v.unsqueeze(2).to_broadcast([SQ, NB, E])

            def pick(p, top, first, oh):
                link(dve.tensor_reduce(top, p[:, :, :], AX.X, ALU.max))
                link(dve.tensor_tensor(eq[:, :, :], p[:, :, :], over_e(top), ALU.is_equal))
                link(dve.tensor_tensor(cand[:, :, :], eq[:, :, :], down8[:, :, :], ALU.mult))
                link(dve.tensor_reduce(first[:, :], cand[:, :, :], AX.X, ALU.max))
                link(dve.tensor_tensor(oh[:, :, :], down8[:, :, :], over_e(first[:, :]), ALU.is_equal))

            shared_act(0, 0)
            x2T_lo(NB - 1)
            shared_act(0, 1)
            sg_lo(2)
            dve.wait_ge(s["lg"], 1)
            dve.wait_ge(s["const"], 4)
            lg = A[0:SQ, 0:NB * E].rearrange("p (b e) -> p b e", e=E)
            link(dve.tensor_reduce(lmax[:, :], lg, AX.X, ALU.max))
            dve.tensor_tensor(logit[:, :, :], lg, over_e(lmax[:, :]), ALU.subtract).then_inc(s["rt"], 1)
            dve.wait_ge(s["lexp"], 1)
            link(dve.tensor_reduce(lsum[:, :], pexp[:, :, :], AX.X, ALU.add))
            link(dve.reciprocal(lrec[:, :], lsum[:, :]))
            link(dve.tensor_tensor(prb[:, :, :], pexp[:, :, :], over_e(lrec[:, :]), ALU.mult))
            pick(prb, topw[:, 0, :], first1, oh1)
            link(dve.scalar_tensor_tensor(out=prb2[:, :, :], in0=oh1[:, :, :], scalar=-2.0, in1=prb[:, :, :],
                                          op0=ALU.mult, op1=ALU.add))
            pick(prb2, topw[:, 1, :], first2, oh2)
            link(dve.tensor_tensor(picked[:, 0:NB, :], oh1[:, :, :], oh2[:, :, :], ALU.add))
            for b in range(NB):
                last = dve.tensor_tensor(before[:, b + 1, :], before[:, b, :], picked[:, b, :], ALU.add)
                if b < NB - 1:
                    link(last)
            last.then_inc(s["trip"], 1)
            add_shared(0, 0)
            shared_act(1, 0)
            add_shared(0, 1)
            shared_act(1, 1)
            sg_lo(3)
            sd_lo(2)
            dve.wait_ge(s["rank"], 2)
            dve.tensor_copy(rank[:, :, :], A[0:SQ, 0:NB * E].rearrange("p (b e) -> p b e", e=E)).then_inc(s["rk"], 1)
            dve.tensor_copy(count[:, :], A[:, NB * E:(NB + 1) * E]).then_inc(s["rk"], 1)
            dve.wait_ge(s["rk"], 2)
            link(dve.tensor_tensor(overs[:, :, :], count[:, :].unsqueeze(2).to_broadcast([P, E, T // P]),
                                   thresh[:, :, :], ALU.is_gt))
            link(dve.tensor_reduce(tiles[:, :], overs[:, :, :], AX.X, ALU.add))
            link(dve.tensor_tensor(tilesb[:, :, :], tiles[:, :].unsqueeze(1).to_broadcast([P, E, E]),
                                   below[:, :, :], ALU.mult))
            link(dve.tensor_reduce(base[:, :], tilesb[:, :, :], AX.X, ALU.add))
            link(dve.scalar_tensor_tensor(out=slot[:, :, :], in0=base[0:SQ, :].unsqueeze(1).to_broadcast([SQ, NB, E]),
                                          scalar=float(P), in1=rank[:, :, :],
                                          op0=ALU.mult, op1=ALU.add))
            link(dve.tensor_tensor(slot1[:, :, :], slot[:, :, :], oh1[:, :, :], ALU.mult))
            link(dve.tensor_tensor(slot2[:, :, :], slot[:, :, :], oh2[:, :, :], ALU.mult))
            with nc.allow_low_precision(reason="slots are whole numbers under 2^24, exact in both types"):
                dve.tensor_reduce(slot_i[:, 0, :], slot1[:, :, :], AX.X, ALU.add).then_inc(s["pos"], 1)
                dve.tensor_reduce(slot_i[:, 1, :], slot2[:, :, :], AX.X, ALU.add).then_inc(s["pos"], 1)
            link(dve.tensor_tensor(started[:, :, :], tile_no[:, :, :], base[0:1, :].unsqueeze(1).to_broadcast([1, NT, E]),
                                   ALU.is_ge))
            link(dve.tensor_reduce(eid_f[:, :], started[:, :, :], AX.X, ALU.add))
            link(dve.scalar_tensor_tensor(out=pair_f[:, :], in0=eid_f[:, 1:NT], scalar=float(E), in1=eid_f[:, 0:NT - 1],
                                          op0=ALU.mult, op1=ALU.add))
            dve.tensor_scalar(eid2[:, :], pair_f[:, :], -1.0 - E, None, ALU.add).then_inc(s["pos"], 1)
            dve.tensor_scalar(eid[:, :], eid_f[:, :], -1.0, None, ALU.add).then_inc(s["pos"], 1)
            for j in range(2, NJ):
                for t in range(NBLK):
                    add_shared(j - 1, t)
                    shared_act(j, t)
                if j + 2 < NJ:
                    sg_lo(j + 2)
                if j + 1 < NJ:
                    sd_lo(j + 1)
            add_shared(NJ - 1, 0)

            def xs_lo(i):
                lo(xsT, as_chunks(S[2], P), "xs_hi", i + 1, "xs_lo", (whole, whole, whole))

            def expert(i):
                return dve.value_load(eid[0:1, bass.ds(i, 1)], min_val=0, max_val=E - 1)

            def experts(i):
                both_ = dve.value_load(eid2[0:1, bass.ds(i, 1)], min_val=0, max_val=E * E - 1)
                return both_ % E, both_ // E

            def gu_lo(e, i, c):
                lo(gu2, w_gu[:, bass.ds(e * GU + c * 2 * F, 2 * F)], "gu_hi", C * i + c + 1, "gu_lo", (whole, c, whole))

            def dn_lo(e, i):
                lo(dn2, w_dn[:, bass.ds(e * DN, H)], "dn_hi", 2 * i + 1, "dn_lo", (whole, 0, whole))

            def expert_act(i):
                dve.wait_ge(s["esil"], i + 1)
                dve.tensor_tensor(act_e[:, 0:F], S[1][:, 0:F], silu_e[:, :], ALU.mult).then_inc(s["eact"], 1)

            def aT_lo(i):
                lo(actT_e, S[3][:, 0:len(FK) * P].rearrange("p (k t) -> p k t", t=P), "aT_hi", i + 1, "aT_lo",
                   (whole, whole, whole))

            def step_e(i):
                e, e_next = experts(i)
                for c in range(C - 1):
                    gu_lo(e_next, i + 1, c)
                expert_act(i)
                xs_lo(i + 1)
                gu_lo(e_next, i + 1, C - 1)
                dn_lo(e, i)
                aT_lo(i)

            dve.memset(act_e[:, F:len(FK) * P], 0.0).then_inc(s["pad_act"], 1)
            xs_lo(0)
            for c in range(C - 1):
                gu_lo(expert(0), 0, c)
            add_shared(NJ - 1, 1)
            gu_lo(expert(0), 0, C - 1)
            step_e(0)
            with dve.Fori(1, NT - 1) as i:
                step_e(i)
            expert_act(NT - 1)
            dn_lo(expert(NT - 1), NT - 1)
            aT_lo(NT - 1)

            for b in range(NB):
                dve.wait_ge(s_gat[b], 16 * TOPK)
                link(dve.scalar_tensor_tensor(out=xres[:, b, :], in0=y_tok[:, b, 0, :], scalar=topw[:, 0, b:b + 1],
                                              in1=xres[:, b, :], op0=ALU.mult, op1=ALU.add))
                dve.scalar_tensor_tensor(out=xres[:, b, :], in0=y_tok[:, b, 1, :], scalar=topw[:, 1, b:b + 1],
                                         in1=xres[:, b, :], op0=ALU.mult, op1=ALU.add).then_inc(s["fin"], 1)


def kernel(x, ctx_512, L0_xattn_Wq, L0_xattn_Wkv_expand, L0_xattn_Wout, L0_ffn_gate_weight,
           L0_ffn_gate_up_weights, L0_ffn_down_weights, L0_ffn_shared_gate_up, L0_ffn_shared_down):
    import concourse.bacc as bacc
    from concourse.bass_utils import run_bass_kernel_spmd

    def by_rows(w):
        t = np.swapaxes(np.asarray(w), -1, -2)
        t = t.reshape(*t.shape[:-2], t.shape[-2] // P, P, t.shape[-1])
        return np.swapaxes(t, -3, -2)

    arrays = {
        "x": x,
        "ctxT": np.asarray(ctx_512).transpose(2, 0, 1),
        "wqT": np.asarray(L0_xattn_Wq).T,
        "wkvT": np.asarray(L0_xattn_Wkv_expand).T,
        "woT": np.asarray(L0_xattn_Wout).T,
        "gateT": by_rows(L0_ffn_gate_weight),
        "guT": by_rows(L0_ffn_gate_up_weights),
        "dnT": np.swapaxes(np.asarray(L0_ffn_down_weights), 1, 2),
        "sguT": by_rows(L0_ffn_shared_gate_up),
        "sdnT": np.asarray(L0_ffn_shared_down).T,
    }
    arrays = {n: np.ascontiguousarray(a) for n, a in arrays.items()}
    nc = bacc.Bacc("TRN2", target_bir_lowering=False, num_devices=1, dynamic_dma_scratch_size=8192)
    args = [nc.dram_tensor(n, a.shape, F32, kind="ExternalInput").ap() for n, a in arrays.items()]
    out = nc.dram_tensor("out", x.shape, F32, kind="ExternalOutput").ap()
    build(nc, *args, out)
    result = run_bass_kernel_spmd(nc, [arrays], core_ids=[0])
    return result.results[0]["out"]
```

```python
import numpy as np
import concourse.bass as bass
from concourse import mybir
from concourse.alu_op_type import AluOpType as ALU

ACT = mybir.ActivationFunctionType
F32 = mybir.dt.float32
U32 = mybir.dt.uint32
I32 = mybir.dt.int32
F32R = mybir.dt.float32r
AX = mybir.AxisListType

P = 128
LN_EPS = 1e-5
MASKED = -3.0e38


class SbufMap:

    def __init__(self, nc):
        self.nc = nc
        self.at = -(-nc.sbuf_base // 32) * 32

    def region(self, nbytes):
        start, self.at = self.at, self.at + -(-nbytes // 32) * 32
        assert self.at <= self.nc.sbuf_usable_end, self.at
        return start

    def tensor(self, name, shape, dtype=F32):
        return self.inside([self.region(4 * int(np.prod(shape[1:]))), None], name, shape, dtype)

    def inside(self, cursor, name, shape, dtype=F32):
        nbytes = -(-4 * int(np.prod(shape[1:])) // 32) * 32
        t = self.nc.alloc_sbuf_tensor_at(name, shape, dtype, offset=cursor[0])
        cursor[0] += nbytes
        assert cursor[1] is None or cursor[0] <= cursor[1], name
        return t


def build(nc, x, ctxT, wqT, wkvT, woT, gateT, guT, dnT, sguT, sdnT, out):
    NB, SQ, H = x.shape
    L = ctxT.shape[0]
    C = H // P
    HD = 32
    NH = H // HD
    R = P // HD
    E = guT.shape[0]
    F = dnT.shape[1]
    FS = sdnT.shape[0]
    T = NB * SQ
    TOPK = 2
    NT = (TOPK * T + E * (P - 1)) // P
    FK = [(k, min(P, F - k)) for k in range(0, F, P)]
    FSK = [(k, min(P, FS - k)) for k in range(0, FS, P)]
    NJ = len(FSK)
    SCALE = float(np.float32(1.0) / np.sqrt(np.float32(HD)))
    assert L == P and NT == 21 and NB == 8 and R == 4

    m = SbufMap(nc)
    GU, DN = C * 2 * F, len(FK) * H
    w_exp_at = m.region(4 * E * (GU + DN))
    w_gu = nc.alloc_sbuf_tensor_at("w_gu", [P, E * GU], F32, offset=w_exp_at)
    w_dn = nc.alloc_sbuf_tensor_at("w_dn", [P, E * DN], F32, offset=w_exp_at + 4 * E * GU)
    shared_at = m.region(4 * 2 * (C * 2 * F + len(FK) * H))
    shared_end = m.at
    xres = m.tensor("xres", [SQ, NB, H])
    x2T_at = m.region(4 * C * T)
    ident = m.tensor("ident", [P, P])
    small = [m.at, nc.sbuf_usable_end]

    def loaded_and_split(cursor, name, shape):
        at = cursor[0]
        raw = m.inside(cursor, name, shape)
        lo = nc.alloc_sbuf_tensor_at(name + "_lo", shape, F32R, offset=at)
        return raw, (m.inside(cursor, name + "_hi", shape, F32R), lo)

    w_gate, w_gate2 = loaded_and_split(small, "w_gate", [P, C, E])

    BLK = 4
    NBLK = NB // BLK
    W = BLK * SQ
    sh = [shared_at, shared_end]
    w_sg, w_sg2 = zip(*(loaded_and_split(sh, f"w_sg{i}", [P, C, 2 * P]) for i in range(2)))
    sg_end = sh[0]
    act_at = shared_end - 2 * 4 * 2 * H - 3 * 4 * W
    act_s, act_s2, silu_s = [None] * NBLK, [None] * NBLK, [None] * NBLK
    act0_at = small[0]
    for t, cursor in enumerate((small, [act_at, shared_end])):
        act_s[t], act_s2[t] = loaded_and_split(cursor, f"act_s{t}", [P, W])
        silu_s[t] = m.inside(cursor, f"silu_s{t}", [P, W])
    sh = [shared_end - 2 * 4 * 2 * H, shared_end]
    w_sd, w_sd2 = zip(*(loaded_and_split(sh, f"w_sd{i}", [P, H]) for i in range(2)))
    lgT = m.inside(small, "lgT", [E, T])

    att = [w_exp_at, shared_at]
    wq_at = att[1] - 2 * 4 * C * H
    w_q, w_q2 = loaded_and_split([wq_at, att[1]], "w_q", [P, C, H])
    w_kv, w_kv2 = loaded_and_split(att, "w_kv", [P, 2 * H])
    w_o, w_o2 = loaded_and_split(att, "w_o", [P, C, H])
    ctx, ctx2 = loaded_and_split(att, "ctx", [P, NB, SQ])
    mask = m.inside(att, "mask", [SQ, C, SQ])
    xn = [m.inside(att, f"xn{i}", [SQ, H]) for i in range(2)]
    xnT = []
    for k, cursor in enumerate((att, [x2T_at, x2T_at + 4 * C * T])):
        xnT.append(tuple(m.inside(cursor, f"xnT{k}_{part}", [P, C, W], F32R) for part in ("hi", "lo")))
    qT = [m.inside(att, f"qT{i}", [P, C, W]) for i in range(NBLK)]
    kT = [m.inside(att, f"kT{i}", [P, C, W]) for i in range(NBLK)]
    v_sb = m.inside(att, "v_sb", [SQ, H])
    score_at = [sg_end, shared_end - 2 * 4 * 2 * H]
    score = [m.inside(score_at, f"score{r}", [SQ, C, SQ]) for r in range(R)]
    prob = [m.inside(att, f"prob{r}", [SQ, C, SQ]) for r in range(R)]
    probT = [m.inside(att, f"probT{r}", [SQ, C, SQ]) for r in range(R)]
    oT = tuple(nc.alloc_sbuf_tensor_at(f"oT_{part}", [P, C, SQ], F32R, offset=at)
               for part, at in (("hi", act0_at), ("lo", act0_at + 4 * W)))
    x2T = (nc.alloc_sbuf_tensor_at("x2T_hi", [P, C, T], F32R, offset=x2T_at),
           nc.alloc_sbuf_tensor_at("x2T_lo", [P, C, T], F32R, offset=wq_at))
    keep = [att[0], wq_at]
    keep_from = keep[0]
    x2n = m.inside(keep, "x2n", [SQ, NB, H])
    dn_end = [w_exp_at + 4 * (E * GU + (e + 1) * DN) for e in range(E)]
    n_early = sum(end <= keep_from for end in dn_end)
    n_late = sum(end > wq_at for end in dn_end)
    loop = [x2T_at, x2T_at + 4 * C * T]
    pair = lambda cursor, name, shape: tuple(m.inside(cursor, f"{name}_{part}", shape, F32R) for part in ("hi", "lo"))
    xsT = pair(loop, "xsT", [P, C, P])
    silu_e = m.inside(loop, "silu_e", [P, F])
    act_e = m.inside(loop, "act_e", [P, len(FK) * P])
    actT_e = pair(loop, "actT_e", [P, len(FK), P])
    y_sb = [m.inside(loop, f"y_sb{i}", [P, H]) for i in range(2)]
    parts = [shared_at, shared_end]
    gu2 = pair(parts, "gu", [P, C, 2 * F])
    dn2 = pair(parts, "dn", [P, len(FK), H])

    sb = lambda name, shape, dtype=F32: m.inside(small, name, shape, dtype)
    xs_in = sb("xs_in", [P, H])
    zeros = xs_in
    negmax = sb("negmax", [SQ, R, C])
    rowsum = sb("rowsum", [SQ, R, C])
    rrow = sb("rrow", [SQ, R, C])
    bn1, mv1, var1, rstd1 = (sb(n, [SQ, NB, k]) for n, k in (("bn1", 6), ("mv1", 2), ("var1", 1), ("rstd1", 1)))
    bn2, mv2, var2, rstd2 = (sb(n, [SQ, NB, k]) for n, k in (("bn2", 6), ("mv2", 2), ("var2", 1), ("rstd2", 1)))
    minus_half = sb("minus_half", [SQ, 1])
    sb = lambda name, shape, dtype=F32: m.inside(keep, name, shape, dtype)
    tri = sb("tri", [SQ, SQ])
    ones = sb("ones", [SQ, P])
    down8 = sb("down8", [SQ, NB, E])
    below = sb("below", [P, E, E])
    thresh = sb("thresh", [P, E, T // P])
    tile_no = sb("tile_no", [1, NT, E])
    rt = lambda name: sb(name, [SQ, NB, E])
    logit, pexp, prb, eq, cand, oh1, oh2, prb2 = (rt(n) for n in "logit pexp prb eq cand oh1 oh2 prb2".split())
    rv = lambda name: sb(name, [SQ, NB])
    lmax, lsum, lrec, first1, first2 = (rv(n) for n in "lmax lsum lrec first1 first2".split())
    picked = sb("picked", [SQ, NB + 1, E])
    before = sb("before", [SQ, NB + 1, E])
    count = sb("count", [P, E])
    overs = sb("over", [P, E, T // P])
    tiles = sb("tiles", [P, E])
    tilesb = sb("tilesb", [P, E, E])
    base = sb("base", [P, E])
    rank = rt("rank")
    slot = rt("slot")
    slot1 = rt("slot1")
    slot2 = rt("slot2")
    slot_i = m.inside(small, "slot_i", [SQ, TOPK, NB], U32)
    started = sb("started", [1, NT, E])
    eid_f = sb("eid_f", [1, NT])
    pair_f = sb("pair_f", [1, NT - 1])
    eid = m.inside(small, "eid", [1, NT], I32)
    dest_pad = m.inside(small, "dest_pad", [NT, P, 2], I32)
    dest_tok = m.inside(small, "dest_tok", [SQ, TOPK, NB, 2], I32)
    topw = dest_tok[:, :, :, 1].bitcast(F32)
    dest = m.inside(small, "dest", [P, NT, 2], U32)
    dest_i = [m.inside(small, f"dest_i{i}", [P, 2], U32) for i in range(2)]
    eid2 = m.inside(small, "eid2", [1, NT - 1], I32)

    bank = [nc.alloc_psum_tensor(f"bank{i}", [P, 512], F32) for i in range(8)]
    S = bank[0:4]
    A, B, CC, D = bank[4:8]

    xs_dram = nc.dram_tensor("xs_dram", [NT * P, H], F32, kind="Internal")
    dest_dram = nc.dram_tensor("dest_dram", [NT * P, 2], U32, kind="Internal")
    sum_dram = nc.dram_tensor("sum_dram", [T + P, H], F32, kind="Internal")

    names = (
        "x0 x0b xrest wq wkv wo wgate ctx0 ctx1 wsg0 wsg1 wsd0 wsd1 we we_late "
        "const zt sel zero "
        "ctx_hi ctx_lo wkv_hi wkv_lo wkv_lo2 wq_hi wq_lo wq_lo2 wo_hi wo_lo wg_hi wg_lo wsg_hi wsg_lo wsd_hi wsd_lo "
        "bs1 st1 rs1a rs1b xn T1 xnT_hi xnT_lo Q QT K KT V Vs "
        "S ms mask exp rr prob prob3 PT probT O oT_hi oT_lo "
        "op x1 bs2 st2 rs2a rs2b x2n T2 x2T_hi x2T_lo "
        "lgT lgs lg rt rtc lexp trip rank rk pos scat dinit dfill ysum0 dscat dest dest_i "
        "sg ssil sact sact_hi sact_lo sdn sres "
        "pad pad_act xin Tx xs_hi xs_lo gu_hi gu_lo dn_hi dn_hi2 dn_lo dn_lo2 dn_lo_end eg esil eact Ta aT_hi aT_lo edn ey yst out").split()
    s = {n: nc.alloc_semaphore(f"s_{n}") for n in names}

    def wait_alone(eng, sem, value):
        eng.wait_ge(sem, value)
        eng.nop(nofuse=True)

    with nc.Block() as block:

        @block.sync
        def _(sp):
            def load_ctx(k):
                at = slice(k * BLK, (k + 1) * BLK)
                sp.dma_start(ctx[:, at, :], ctxT[:, at, 0:SQ]).then_inc(s[f"ctx{k}"], 16)

            load_ctx(0)
            sp.dma_start(xres[:, 0, :], x[0]).then_inc(s["x0"], 16)
            sp.dma_start(w_kv[:, :], wkvT).then_inc(s["wkv"], 16)
            sp.dma_start(xres[:, 1:BLK, :], x[1:BLK].rearrange("b q d -> q b d")).then_inc(s["x0b"], 16)
            sp.dma_start(w_q[:, :, :], wqT.rearrange("(c p) d -> p c d", p=P)).then_inc(s["wq"], 16)
            sp.dma_start(xres[:, BLK:NB, :], x[BLK:NB].rearrange("b q d -> q b d")).then_inc(s["xrest"], 16)
            load_ctx(1)
            sp.dma_start(w_o[:, :, :], woT.rearrange("(c p) d -> p c d", p=P)).then_inc(s["wo"], 16)
            sp.dma_start(w_gate[:, :, :], gateT).then_inc(s["wgate"], 16)

            def load_sg(j):
                k, w = FSK[j]
                for n in range(2):
                    sp.dma_start(w_sg[j % 2][:, :, n * w:(n + 1) * w], sguT[:, :, n * FS + k:n * FS + k + w])\
                        .then_inc(s[f"wsg{j % 2}"], 16)

            def load_sd(j):
                k, w = FSK[j]
                sp.dma_start(w_sd[j % 2][0:w, :], sdnT[k:k + w, :]).then_inc(s[f"wsd{j % 2}"], 16)

            for j in range(2):
                load_sg(j)
                load_sd(j)
            sp.wait_ge(s["dinit"], 2)
            sp.dma_start(dest_dram[:, :].rearrange("(n p) o -> n (p o)", p=P),
                         dest_pad[:, :, :].bitcast(U32).rearrange("n p o -> n (p o)")).then_inc(s["dfill"], 16)
            sp.wait_ge(s["zt"], 1)
            sp.dma_start(xs_dram[:, :].rearrange("(n p) d -> p n d", p=P),
                         zeros[:, :].unsqueeze(1).to_broadcast([P, NT, H])).then_inc(s["zero"], 16)
            sp.dma_start(sum_dram[T:T + P, :], zeros[:, :]).then_inc(s["ysum0"], 16)

            def load_gu(e, sem):
                sp.dma_start(w_gu[:, e * GU:(e + 1) * GU], guT[e].rearrange("p c f -> p (c f)")).then_inc(sem, 16)

            def load_dn(e, sem):
                k2 = F // P * P
                at = w_dn[:, e * DN:(e + 1) * DN].rearrange("p (k d) -> p k d", d=H)
                sp.dma_start(at[:, 0:k2 // P, :],
                             dnT[e, 0:k2, :].rearrange("(k p) d -> p k d", p=P)).then_inc(sem, 16)
                sp.dma_start(at[0:F - k2, k2 // P, :], dnT[e, k2:F, :]).then_inc(sem, 16)

            sp.wait_ge(s["op"], NB)

            def next_sg(j):
                sp.wait_ge(s["sg"], NBLK * (j - 1))
                load_sg(j)

            def next_sd(j):
                sp.wait_ge(s["sdn"], NB * (j - 1))
                load_sd(j)

            def load_x(i):
                sp.dma_start(xs_in[:, :], xs_dram[bass.ds(i * P, P), :]).then_inc(s["xin"], 16)

            for e in range(0, 2):
                load_gu(e, s["we"])
            next_sg(2)
            for e in range(2, 5):
                load_gu(e, s["we"])
            next_sg(3)
            next_sd(2)
            for e in range(5, E):
                load_gu(e, s["we"])
            for e in range(n_early):
                load_dn(e, s["we"])
            next_sg(4)
            next_sd(3)
            next_sg(5)
            next_sd(4)
            sp.wait_ge(s["pos"], 4)
            sp.wait_ge(s["scat"], 16 * TOPK * NB)
            sp.wait_ge(s["ysum0"], 16)
            load_x(0)
            for e in range(n_early, E - n_late):
                load_dn(e, s["we"])
            next_sd(5)
            sp.wait_ge(s["dscat"], 16 * TOPK * NB)
            sp.dma_start(dest[:, :, :], dest_dram[:, :].rearrange("(n p) o -> p n o", p=P),
                         allow_slow_non_contiguous=True).then_inc(s["dest"], 16)
            sp.wait_ge(s["sg"], NBLK * NJ)
            for e in range(E - n_late, E):
                load_dn(e, s["we_late"])

            sp.wait_ge(s["Tx"], 1)
            load_x(1)
            def start_sum(b0, b1):
                sp.dma_start(sum_dram[b0 * SQ:b1 * SQ, :].rearrange("(b q) d -> q b d", q=SQ), xres[:, b0:b1, :])\
                    .then_inc(s["ysum0"], 16)

            sp.wait_ge(s["sres"], NB * NJ - BLK + 1)
            start_sum(0, NB - BLK)
            start_sum(NB - 1, NB)
            sp.wait_ge(s["Tx"], 2)
            load_x(2)
            sp.wait_ge(s["sres"], NB * NJ)
            start_sum(NB - BLK, NB - 1)
            with sp.Fori(3, NT) as i:
                sp.wait_ge(s["Tx"], i)
                load_x(i)
            sp.wait_ge(s["yst"], 16 * NT)
            sp.dma_start(out.rearrange("b q d -> (b q) d").rearrange("(p n) d -> p (n d)", p=P),
                         sum_dram[0:T, :].rearrange("(p n) d -> p (n d)", p=P)).then_inc(s["out"], 16)
            sp.wait_ge(s["out"], 16)

        @block.gpsimd
        def _(pool):
            cnt = [0]

            def own(ins):
                cnt[0] += 1
                ins.then_inc(s["sel"], 1)
                pool.wait_ge(s["sel"], cnt[0])

            own(pool.memset(ident[:, :], 0.0))
            pool.affine_select(out=ident[:, :], in_=ident[:, :], compare_op=ALU.not_equal, fill=1.0, base=0,
                               pattern=[[-1, P]], channel_multiplier=1).then_inc(s["const"], 1)
            pool.memset(minus_half[:, :], -0.5).then_inc(s["const"], 1)
            pool.memset(zeros[:, :], 0.0).then_inc(s["zt"], 1)
            own(pool.memset(dest_pad[:, :, :].bitcast(F32), 0.0))
            pool.iota(dest_pad[:, :, 0], [[1, P]], base=T, channel_multiplier=0).then_inc(s["dinit"], 1)
            pool.iota(dest_tok[:, :, :, 0], [[0, TOPK], [SQ, NB]], base=0, channel_multiplier=1)\
                .then_inc(s["dinit"], 1)
            own(pool.memset(mask[:, :, :], 0.0))
            pool.affine_select(out=mask[:, :, :], in_=mask[:, :, :], compare_op=ALU.is_ge, fill=MASKED, base=0,
                               pattern=[[0, C], [-1, SQ]], channel_multiplier=1).then_inc(s["const"], 1)
            pool.wait_ge(s["const"], 3)

            def normalised(b):
                r = R - 1
                pool.wait_ge(s["rr"], R * (b + 1))
                pool.tensor_tensor(prob[r][:, :, :], prob[r][:, :, :],
                                   rrow[:, r, :].unsqueeze(2).to_broadcast([SQ, C, SQ]), ALU.mult)\
                    .then_inc(s["prob3"], 1)

            def rstd(n, stats, var, rs, mv, own_sem, done):
                pool.wait_ge(s[stats], n + 1)
                pool.tensor_scalar(var[:, n, :], mv[:, n, 1:2], LN_EPS, 1.0, ALU.add, ALU.mult).then_inc(s[own_sem], 1)
                pool.wait_ge(s[own_sem], n + 1)
                pool.tensor_tensor(rs[:, n, :], var[:, n, :], minus_half[:, :], ALU.pow).then_inc(s[done], 1)

            rstd(0, "st1", var1, rstd1, mv1, "rs1a", "rs1b")
            pool.wait_ge(s["wkv_hi"], 1)
            pool.tensor_tensor(w_kv2[1][:, H:2 * H], w_kv[:, H:2 * H], w_kv2[0][:, H:2 * H].bitcast(F32), ALU.subtract)\
                .then_inc(s["wkv_lo2"], 1)
            for n in range(1, BLK):
                rstd(n, "st1", var1, rstd1, mv1, "rs1a", "rs1b")
            pool.wait_ge(s["wq_hi"], 1)
            half = slice(C // 2, C)
            pool.tensor_tensor(w_q2[1][:, half, :], w_q[:, half, :], w_q2[0][:, half, :].bitcast(F32), ALU.subtract)\
                .then_inc(s["wq_lo2"], 1)
            for n in range(BLK, NB):
                rstd(n, "st1", var1, rstd1, mv1, "rs1a", "rs1b")
            pool.wait_ge(s["wo"], 16)
            pool.tensor_copy(w_o2[0][:, :, :], w_o[:, :, :]).then_inc(s["wo_hi"], 1)
            pool.wait_ge(s["wo_hi"], 1)
            pool.tensor_tensor(w_o2[1][:, :, :], w_o[:, :, :], w_o2[0][:, :, :].bitcast(F32), ALU.subtract)\
                .then_inc(s["wo_lo"], 1)
            own(pool.memset(tri[:, :], 1.0))
            own(pool.affine_select(out=tri[:, :], in_=tri[:, :], compare_op=ALU.is_gt, fill=0.0, base=0,
                                   pattern=[[1, SQ]], channel_multiplier=-1))
            own(pool.memset(ones[:, :], 1.0))
            own(pool.iota(down8[:, :, :], [[0, NB], [-1, E]], base=E, channel_multiplier=0,
                          allow_small_or_imprecise_dtypes=True))
            own(pool.memset(below[:, :, :], 1.0))
            own(pool.affine_select(out=below[:, :, :], in_=below[:, :, :], compare_op=ALU.is_gt, fill=0.0, base=0,
                                   pattern=[[1, E], [-1, E]], channel_multiplier=0))
            own(pool.iota(thresh[:, :, :], [[0, E], [P, T // P]], base=0, channel_multiplier=0,
                          allow_small_or_imprecise_dtypes=True))
            own(pool.iota(tile_no[:, :, :], [[1, NT], [0, E]], base=0, channel_multiplier=0,
                          allow_small_or_imprecise_dtypes=True))
            pool.memset(before[:, 0:1, :], 0.0).then_inc(s["const"], 1)
            normalised(0)
            for n in range(1, NB):
                if n >= 2:
                    rstd(n - 2, "st2", var2, rstd2, mv2, "rs2a", "rs2b")
                normalised(n)
            for n in (NB - 2, NB - 1):
                rstd(n, "st2", var2, rstd2, mv2, "rs2a", "rs2b")

            pool.wait_ge(s["zero"], 16)
            pool.wait_ge(s["x2n"], NB)
            pool.wait_ge(s["pos"], 2)
            for b in range(NB):
                for k in range(TOPK):
                    pool.indirect_dma_start(
                        out=xs_dram[:, :], out_offset=bass.IndirectOffsetOnAxis(ap=slot_i[:, k, b:b + 1], axis=0),
                        in_=x2n[:, b, :], in_offset=None).then_inc(s["scat"], 16)
            pool.wait_ge(s["dfill"], 16)
            for b in range(NB):
                for k in range(TOPK):
                    pool.indirect_dma_start(
                        out=dest_dram[:, :], out_offset=bass.IndirectOffsetOnAxis(ap=slot_i[:, k, b:b + 1], axis=0),
                        in_=dest_tok[:, k, b, :].bitcast(U32), in_offset=None).then_inc(s["dscat"], 16)

            def next_dest(i, turn, first=False):
                if not first:
                    wait_alone(pool, s["yst"], 16 * (i - 1))
                pool.tensor_copy(dest_i[turn][:, :], dest[:, bass.ds(i, 1), :]).then_inc(s["dest_i"], 1)

            def add_y(i, turn, first=False):
                wait_alone(pool, s["dest_i"], i + 1)
                wait_alone(pool, s["ey"], i + 1)
                if first:
                    pool.wait_ge(s["ysum0"], 16 * 4)
                else:
                    wait_alone(pool, s["yst"], 16 * i)
                pool.indirect_dma_start(
                    out=sum_dram[:, :], out_offset=bass.IndirectOffsetOnAxis(ap=dest_i[turn][:, 0:1], axis=0),
                    in_=y_sb[turn][:, :], in_offset=None, compute_op=ALU.add).then_inc(s["yst"], 16)

            def dn_parts(i, turn, first=False, second=False, third=False):
                e = pool.value_load(eid[0:1, bass.ds(i, 1)], min_val=0, max_val=E - 1)
                w = FK[-1][1]
                last = w_dn[0:w, bass.ds(e * DN + 2 * H, H)]
                if not first:
                    next_dest(i - 1, 1 - turn, first=second or third)
                    pool.wait_ge(s["edn"], len(FK) * i - 1)
                pool.tensor_copy(dn2[0][0:w, 2, :], last).then_inc(s["dn_hi2"], 1)
                wait_alone(pool, s["dn_hi2"], i + 1)
                pool.tensor_tensor(dn2[1][0:w, 2, :], last, dn2[0][0:w, 2, :].bitcast(F32), ALU.subtract)\
                    .then_inc(s["dn_lo2"], 1)
                if not first:
                    add_y(i - 1, 1 - turn, first=second)
                wait_alone(pool, s["dn_hi"], 2 * (i + 1))
                pool.tensor_tensor(dn2[1][:, 1, :], w_dn[:, bass.ds(e * DN + H, H)], dn2[0][:, 1, :].bitcast(F32),
                                   ALU.subtract).then_inc(s["dn_lo2"], 1)

            assert len(FK) == 3
            pool.wait_ge(s["pos"], 4)
            pool.wait_ge(s["we"], 16 * (3 * E - 2 * n_late))
            pool.wait_ge(s["we_late"], 16 * 2 * n_late)
            pool.wait_ge(s["sdn"], NB * NJ)
            rest = FK[-1][1]
            for t in (dn2[0], dn2[1]):
                pool.memset(t[rest:P, len(FK) - 1, :].bitcast(F32), 0.0).then_inc(s["pad"], 1)
            pool.wait_ge(s["pad"], 2)
            pool.wait_ge(s["dest"], 16)
            dn_parts(0, 0, first=True)
            dn_parts(1, 1, second=True)
            dn_parts(2, 0, third=True)
            dn_parts(3, 1)
            with pool.Fori(4, NT - 2, 2) as i:
                dn_parts(i, 0)
                dn_parts(i + 1, 1)
            for i in (NT - 2, NT - 1):
                next_dest(i, i % 2)
            for i in (NT - 2, NT - 1):
                add_y(i, i % 2)

        @block.tensor
        def _(pe):
            def transposes(dst, src):
                for c in range(C):
                    ins = pe.transpose(dst[:, c * SQ:(c + 1) * SQ], src[:, c * P:(c + 1) * P], ident[0:SQ, 0:SQ])
                return ins

            def product(dst, terms, start=True, stop=True, first=0, last=None):
                passes = [(a[i], b[j]) for a, b in terms for i, j in ((1, 0), (0, 1), (0, 0))]
                for n, (a, b) in list(enumerate(passes))[first:last]:
                    ins = pe.matmul(dst, a, b, start=start and n == 0, stop=stop and n == len(passes) - 1)
                return ins

            def both(pair, *at):
                return tuple(t[at] for t in pair)

            every = slice(None)

            def t1(n, bank_):
                pe.wait_ge(s["xn"], n + 1)
                transposes(bank_, xn[n % 2]).then_inc(s["T1"], 1)

            def q_proj(k, j, bank_):
                product(bank_[:, 0:W], [(both(w_q2, every, c, slice(j * P, (j + 1) * P)), both(xnT[k], every, c, every))
                                        for c in range(C)]).then_inc(s["Q"], 1)

            def k_proj(k, j, bank_):
                product(bank_[:, 0:W], [(both(w_kv2, every, slice(j * P, (j + 1) * P)),
                                         both(ctx2, every, slice(k * BLK, (k + 1) * BLK), every))]).then_inc(s["K"], 1)

            def v_proj(n):
                product(A[0:SQ, :], [(both(ctx2, every, n, every), both(w_kv2, every, slice(H, 2 * H)))])\
                    .then_inc(s["V"], 1)

            def out_proj(n, first, last):
                pe.wait_ge(s["oT_hi"], n + 1)
                pe.wait_ge(s["oT_lo"], n + 1)
                ins = product(D[0:SQ, :], [(both(oT, every, c, every), both(w_o2, every, c, every))
                                           for c in range(C)], first=first, last=last)
                if last == 3 * C:
                    ins.then_inc(s["op"], 1)

            def t2(n):
                pe.wait_ge(s["x2n"], n + 1)
                for c in range(C):
                    ins = pe.transpose(B[:, c * SQ:(c + 1) * SQ], x2n[:, n, c * P:(c + 1) * P], ident[0:SQ, 0:SQ])
                ins.then_inc(s["T2"], 1)

            def scores(b):
                k, cols = b // BLK, slice(b % BLK * SQ, (b % BLK + 1) * SQ)
                pe.wait_ge(s["QT"], C * (k + 1))
                pe.wait_ge(s["KT"], C * (k + 1))
                order = [(r, c) for c in range(C) for r in range(R)]
                for r, c in sorted(order) if b == 0 else order:
                    rows = slice(HD * r, HD * (r + 1))
                    ins = pe.matmul(S[r][0:SQ, c * SQ:(c + 1) * SQ], qT[k][rows, c, cols], kT[k][rows, c, cols],
                                    start=True, stop=True)
                    if c == C - 1:
                        ins.then_inc(s["S"], 1)

            def shared_gu(j, t, halves=(0, 1)):
                k, w = FSK[j]
                n = NBLK * j + t
                dst = (S[2 * t], S[2 * t + 1])
                if t == 0 and halves[0] == 0:
                    pe.wait_ge(s["wsg_hi"], j + 1)
                    pe.wait_ge(s["wsg_lo"], j + 1)
                if j >= 1:
                    pe.wait_ge(s["sact"], n - NBLK + 1)
                cols = slice(t * W, (t + 1) * W)
                for h in halves[0:-(-2 * w // P)]:
                    ins = product(dst[h][:, 0:W], [(both(w_sg2[j % 2], every, c, slice(h * P, (h + 1) * P)),
                                                    both(x2T, every, c, cols)) for c in range(C)])
                if halves[-1] == 1:
                    ins.then_inc(s["sg"], 1)

            def keep_busy(banks, times):
                with pe.Fori(0, times):
                    for b in banks:
                        pe.transpose(b[:, 0:P], ident[:, :], ident[:, :])

            pe.wait_ge(s["const"], 1)
            keep_busy((A, B, CC, D), 6)
            t1(0, S[0])
            for what in ("ctx_hi", "ctx_lo", "wkv_hi", "wkv_lo"):
                pe.wait_ge(s[what], 1)
            k_proj(0, 0, bank[4])
            for j in range(1, C):
                k_proj(0, j, bank[4 + j])
                t1(j, S[j])
            pe.wait_ge(s["xnT_lo"], 2)
            keep_busy(S[0:2], 5)
            for what, value in (("wq_hi", 2), ("wq_lo", 1), ("wq_lo2", 1), ("xnT_hi", BLK), ("xnT_lo", BLK)):
                pe.wait_ge(s[what], value)
            for j in range(C):
                pe.wait_ge(s["KT"], j + 1)
                q_proj(0, j, bank[4 + j])
                t1(BLK + j, S[j])
            pe.wait_ge(s["wkv_lo2"], 1)
            pe.wait_ge(s["QT"], C - 1)
            v_proj(0)
            pe.wait_ge(s["ctx_hi"], 2)
            pe.wait_ge(s["ctx_lo"], 2)
            k_proj(1, 0, CC)
            pe.wait_ge(s["xnT_hi"], NB)
            pe.wait_ge(s["xnT_lo"], NB)
            scores(0)
            q_proj(1, 0, D)

            def fill(j):
                q_proj(1, j, D)
                k_proj(1, j, CC)

            def fill_next(b):
                pe.wait_ge(s["QT"], C + b + 1)
                if b >= 2:
                    pe.wait_ge(s["x1"], b - 1)
                pe.wait_ge(s["KT"], C + b + 1)
                if b >= 1:
                    pe.wait_ge(s["oT_hi"], b)
                    pe.wait_ge(s["oT_lo"], b)
                fill(b + 1)

            for b in range(NB):
                if b + 1 < NB:
                    pe.wait_ge(s["mask"], R * (b + 1))
                    scores(b + 1)
                else:
                    pe.wait_ge(s["mask"], R * NB)
                    pe.wait_ge(s["x2T_hi"], BLK)
                    pe.wait_ge(s["x2T_lo"], BLK)
                    shared_gu(0, 0, (0,))
                if 1 <= b < C - 1:
                    fill_next(b)
                if b >= 2:
                    t2(b - 2)
                for r in range(R):
                    if r == 2 and b == 0:
                        fill_next(0)
                    if r == 1 and b >= 1:
                        pe.wait_ge(s["QT"], C * NBLK if b >= C - 1 else C + b + 2)
                        if b >= 2:
                            pe.wait_ge(s["x1"], b - 1)
                        if b == 1:
                            pe.wait_ge(s["wo_hi"], 1)
                            pe.wait_ge(s["wo_lo"], 1)
                        out_proj(b - 1, 0, 7)
                    if r == 3 and b >= 1:
                        out_proj(b - 1, 7, 9)
                    if r < R - 1:
                        pe.wait_ge(s["prob"], (R - 1) * b + r + 1)
                    else:
                        pe.wait_ge(s["prob3"], b + 1)
                    if r == 0:
                        pe.wait_ge(s["Vs"], b + 1)
                    if r == 1 and b >= 2:
                        pe.wait_ge(s["x2T_hi"], b - 1)
                        pe.wait_ge(s["x2T_lo"], b - 1)
                    if r >= 2:
                        pe.wait_ge(s["probT"], R * b + r - 1)
                    for c in range(C):
                        ins = pe.transpose((A, B)[r % 2][0:SQ, c * SQ:(c + 1) * SQ], prob[r][:, c, :],
                                           ident[0:SQ, 0:SQ])
                    ins.then_inc(s["PT"], 1)
                if b >= 1:
                    out_proj(b - 1, 9, 3 * C)
                pe.wait_ge(s["KT"], C * NBLK if b >= C - 1 else C + b + 2)
                for h in range(NH):
                    r, c = h % R, h // R
                    if c == 0:
                        pe.wait_ge(s["probT"], R * b + r + 1)
                    ins = pe.matmul(CC[HD * r:HD * (r + 1), c * SQ:(c + 1) * SQ], v_sb[:, h * HD:(h + 1) * HD],
                                    probT[r][:, c, :], start=True, stop=True)
                ins.then_inc(s["O"], 1)
                if b + 1 < NB:
                    v_proj(b + 1)
            shared_gu(0, 0, (1,))
            t2(NB - 2)
            pe.wait_ge(s["x1"], NB - 1)
            out_proj(NB - 1, 0, 3 * C)

            def t_x(i):
                pe.wait_ge(s["xin"], 16 * i + 16)
                for c in range(C):
                    ins = pe.transpose(S[2][:, c * P:(c + 1) * P], xs_in[:, c * P:(c + 1) * P], ident[:, :])
                ins.then_inc(s["Tx"], 1)

            out_bank = (B, CC, D, A)

            def shared_down(j, t):
                k, w = FSK[j]
                pe.wait_ge(s["wsd_hi"], j + 1)
                pe.wait_ge(s["wsd_lo"], j + 1)
                pe.wait_ge(s["sact_hi"], NBLK * j + t + 1)
                pe.wait_ge(s["sact_lo"], NBLK * j + t + 1)
                for i in range(BLK):
                    n = NB * j + t * BLK + i
                    if n >= BLK:
                        pe.wait_ge(s["sres"], n - BLK + 1)
                    if n == BLK - 1:
                        pe.wait_ge(s["rt"], 1)
                    if n == NB + BLK - 1:
                        pe.wait_ge(s["rk"], 2)
                    product(out_bank[i][0:SQ, :], [(both(act_s2[t], slice(0, w), slice(i * SQ, (i + 1) * SQ)),
                                                    both(w_sd2[j % 2], slice(0, w), every))]).then_inc(s["sdn"], 1)

            def logits(t):
                product((CC, D)[t][0:E, 0:W], [(both(w_gate2, every, c, every), both(x2T, every, c, slice(t * W, (t + 1) * W)))
                                               for c in range(C)]).then_inc(s["lgT"], 1)

            pe.wait_ge(s["oT_lo"], NB)
            pe.wait_ge(s["wg_hi"], 1)
            pe.wait_ge(s["wg_lo"], 1)
            logits(0)
            pe.wait_ge(s["x2T_hi"], NB - 1)
            pe.wait_ge(s["x2T_lo"], NB - 1)
            t2(NB - 1)
            shared_gu(1, 0, (0,))
            pe.wait_ge(s["x2T_hi"], NB)
            pe.wait_ge(s["x2T_lo"], NB)
            shared_gu(0, 1)
            pe.wait_ge(s["x1"], NB)
            logits(1)
            shared_gu(1, 0, (1,))
            pe.wait_ge(s["lgs"], NBLK)
            for b in range(NB):
                ins = pe.transpose(A[0:SQ, b * E:(b + 1) * E], lgT[:, b * SQ:(b + 1) * SQ], ident[0:E, 0:E])
            ins.then_inc(s["lg"], 1)
            shared_down(0, 0)
            shared_gu(1, 1)
            shared_down(0, 1)
            shared_gu(2, 0)
            pe.wait_ge(s["trip"], 1)
            pe.wait_ge(s["sres"], NB)
            pe.matmul(A[0:SQ, 0:NB * E], tri[:, :], picked[:, 0:NB, :], start=True, stop=False)
            pe.matmul(A[0:SQ, 0:NB * E], ones[:, 0:SQ], before[:, 0:NB, :], start=False, stop=True).then_inc(s["rank"], 1)
            pe.matmul(A[:, NB * E:(NB + 1) * E], ones[:, :], before[:, NB, :], start=True, stop=True)\
                .then_inc(s["rank"], 1)
            shared_down(1, 0)
            shared_gu(2, 1)
            shared_down(1, 1)
            for j in range(3, NJ):
                shared_gu(j, 0)
                shared_down(j - 1, 0)
                shared_gu(j, 1)
                shared_down(j - 1, 1)
            shared_down(NJ - 1, 0)
            pe.wait_ge(s["sact"], NBLK * NJ)
            t_x(0)
            shared_down(NJ - 1, 1)

            def gate_up(i):
                pe.wait_ge(s["xs_hi"], i + 1)
                pe.wait_ge(s["xs_lo"], i + 1)
                for c in range(C):
                    pe.wait_ge(s["gu_hi"], C * i + c + 1)
                    pe.wait_ge(s["gu_lo"], C * i + c + 1)
                    for n, (x_, w_) in enumerate(((0, 1), (0, 0), (1, 0))):
                        for dst, f0 in ((S[0], 0), (S[1], F)):
                            ins = pe.matmul(dst[:, 0:F], xsT[x_][:, c, :], gu2[w_][:, c, f0:f0 + F],
                                            start=c == 0 and n == 0, stop=c == C - 1 and n == 2)
                    ins.then_inc(s["eg"], 1)

            def down(i, last=False):
                pe.wait_ge(s["aT_hi"], i + 1)
                pe.wait_ge(s["aT_lo"], i + 1)
                for n, j in enumerate((0, 2, 1)):
                    if j == 0:
                        pe.wait_ge(s["dn_hi"], 2 * i + 1)
                        pe.wait_ge(s["dn_lo"], i + 1)
                    elif last:
                        pe.wait_ge(s["dn_lo_end"], n)
                    else:
                        pe.wait_ge(s["dn_lo2"], 2 * i + n)
                    product(A[:, :], [(both(actT_e, every, j, every), both(dn2, every, j, every))],
                            n == 0, n == 2).then_inc(s["edn"], 1)

            def t_act(i):
                pe.wait_ge(s["eact"], i + 1)
                for j in range(len(FK)):
                    ins = pe.transpose(S[3][:, j * P:(j + 1) * P], act_e[:, j * P:(j + 1) * P], ident[:, :])
                ins.then_inc(s["Ta"], 1)

            gate_up(0)
            t_x(1)
            pe.wait_ge(s["sres"], NB * NJ - BLK + 1)
            pe.wait_ge(s["pad"], 2)
            pe.wait_ge(s["pad_act"], 1)
            t_act(0)
            gate_up(1)
            t_x(2)
            down(0)
            t_act(1)
            with pe.Fori(2, NT - 1) as i:
                gate_up(i)
                t_x(i + 1)
                pe.wait_ge(s["ey"], i - 1)
                down(i - 1)
                t_act(i)
            gate_up(NT - 1)
            pe.wait_ge(s["ey"], NT - 2)
            down(NT - 2)
            t_act(NT - 1)
            pe.wait_ge(s["ey"], NT - 1)
            down(NT - 1, last=True)

        @block.scalar
        def _(act):
            def copy_out(dst, src, sem):
                act.activation(dst, src, ACT.Copy).then_inc(s[sem], 1)

            def as_chunks(b, w=SQ, p=P):
                return b[0:p, 0:C * w].rearrange("p (c q) -> p c q", c=C)

            def hi(dst, src, sem):
                copy_out(dst, src, sem)

            def put_xnT(n, bank_):
                act.wait_ge(s["T1"], n + 1)
                at = n % BLK * SQ
                hi(xnT[n // BLK][0][:, :, at:at + SQ], as_chunks(bank_), "xnT_hi")

            def put_qT(k, j, bank_):
                act.wait_ge(s["Q"], C * k + j + 1)
                copy_out(qT[k][:, j, :], bank_[:, 0:W], "QT")

            def put_kT(k, j, bank_):
                act.wait_ge(s["K"], C * k + j + 1)
                copy_out(kT[k][:, j, :], bank_[:, 0:W], "KT")

            def put_v(n):
                act.wait_ge(s["V"], n + 1)
                copy_out(v_sb[:, :], A[0:SQ, :], "Vs")

            def put_x2T(n):
                act.wait_ge(s["T2"], n + 1)
                hi(x2T[0][:, :, n * SQ:(n + 1) * SQ], as_chunks(B), "x2T_hi")

            def sg_hi(j):
                act.wait_ge(s[f"wsg{j % 2}"], 32 * (j // 2 + 1))
                w2 = 2 * FSK[j][1]
                hi(w_sg2[j % 2][0][:, :, 0:w2], w_sg[j % 2][:, :, 0:w2], "wsg_hi")

            def sd_hi(j):
                act.wait_ge(s[f"wsd{j % 2}"], 16 * (j // 2 + 1))
                w = FSK[j][1]
                hi(w_sd2[j % 2][0][0:w, :], w_sd[j % 2][0:w, :], "wsd_hi")

            def exps(b, r):
                act.wait_ge(s["mask"], R * b + r + 1)
                if b >= 1:
                    act.wait_ge(s["PT"], R * (b - 1) + r + 1)
                for c in range(C):
                    ins = act.activation(prob[r][:, c, :], score[r][:, c, :], ACT.Exp, bias=negmax[:, r, c:c + 1],
                                         accum_out=rowsum[:, r, c:c + 1])
                ins.then_inc(s["exp"], 1)

            def put_pT(b, r):
                act.wait_ge(s["PT"], R * b + r + 1)
                copy_out(probT[r][:, :, :], as_chunks((A, B)[r % 2], p=SQ), "probT")

            def ctx_hi(k):
                act.wait_ge(s[f"ctx{k}"], 16)
                at = slice(k * BLK, (k + 1) * BLK)
                hi(ctx2[0][:, at, :], ctx[:, at, :], "ctx_hi")

            ctx_hi(0)
            act.wait_ge(s["wkv"], 16)
            hi(w_kv2[0][:, :], w_kv[:, :], "wkv_hi")
            put_xnT(0, S[0])
            put_kT(0, 0, bank[4])
            act.wait_ge(s["wq"], 16)
            for j in range(1, C):
                if j <= 2:
                    at = slice((2 - j) * C // 2, (3 - j) * C // 2)
                    hi(w_q2[0][:, at, :], w_q[:, at, :], "wq_hi")
                put_kT(0, j, bank[4 + j])
                put_xnT(j, S[j])
            ctx_hi(1)
            for j in range(C):
                put_qT(0, j, bank[4 + j])
                put_xnT(BLK + j, S[j])
            for r in range(R):
                exps(0, r)
            put_v(0)
            put_kT(1, 0, CC)
            put_qT(1, 0, D)
            for b in range(NB):
                if 1 <= b < C - 1:
                    put_qT(1, b + 1, D)
                    put_kT(1, b + 1, CC)
                if b >= 2:
                    put_x2T(b - 2)
                if b == 2:
                    act.wait_ge(s["wgate"], 16)
                    hi(w_gate2[0][:, :, :], w_gate[:, :, :], "wg_hi")
                put_pT(b, 0)
                if b == 0:
                    put_pT(b, 1)
                if b + 1 < NB:
                    exps(b + 1, 0)
                if b == 0:
                    put_qT(1, 1, D)
                    put_kT(1, 1, CC)
                for r in range(2 if b == 0 else 1, R):
                    put_pT(b, r)
                if b + 1 < NB:
                    exps(b + 1, 1)
                if b == NB - 1:
                    sg_hi(1)
                    sd_hi(1)
                act.wait_ge(s["O"], b + 1)
                hi(oT[0][:, :, :], as_chunks(CC), "oT_hi")
                if b + 1 < NB:
                    put_v(b + 1)
                    exps(b + 1, 2)
                    exps(b + 1, 3)
                if b == 0:
                    sg_hi(0)
                    sd_hi(0)

            def shared_silu(j, t):
                w = FSK[j][1]
                act.wait_ge(s["sg"], NBLK * j + t + 1)
                act.activation(silu_s[t][0:w, :], S[2 * t][0:w, 0:W], ACT.Silu).then_inc(s["ssil"], 1)

            def shared_hi(j, t):
                w = FSK[j][1]
                n = NBLK * j + t
                if j >= 1:
                    act.wait_ge(s["sdn"], NB * (j - 1) + BLK * (t + 1))
                act.wait_ge(s["sact"], n + 1)
                hi(act_s2[t][0][0:w, :], act_s[t][0:w, :], "sact_hi")

            def put_logits(t):
                act.wait_ge(s["lgT"], t + 1)
                copy_out(lgT[:, t * W:(t + 1) * W], (CC, D)[t][0:E, 0:W], "lgs")

            put_x2T(NB - 2)
            shared_silu(0, 0)
            shared_hi(0, 0)
            put_x2T(NB - 1)
            put_logits(0)
            shared_silu(0, 1)
            shared_hi(0, 1)
            put_logits(1)
            sg_hi(2)
            shared_silu(1, 0)
            act.wait_ge(s["rt"], 1)
            act.activation(pexp[:, :, :], logit[:, :, :], ACT.Exp).then_inc(s["lexp"], 1)
            shared_hi(1, 0)
            shared_silu(1, 1)
            shared_hi(1, 1)
            sg_hi(3)
            sd_hi(2)
            for j in range(2, NJ):
                shared_silu(j, 0)
                shared_hi(j, 0)
                shared_silu(j, 1)
                shared_hi(j, 1)
                if j + 2 < NJ:
                    sg_hi(j + 2)
                if j + 1 < NJ:
                    sd_hi(j + 1)

            def xs_hi(i):
                act.wait_ge(s["Tx"], i + 1)
                hi(xsT[0][:, :, :], as_chunks(S[2], w=P), "xs_hi")

            def expert(i):
                return act.value_load(eid[0:1, bass.ds(i, 1)], min_val=0, max_val=E - 1)

            def experts(i):
                both_ = act.value_load(eid2[0:1, bass.ds(i, 1)], min_val=0, max_val=E * E - 1)
                return both_ % E, both_ // E

            def gu_hi(e, i, c, first=False):
                if not first:
                    act.wait_ge(s["eg"], C * (i - 1) + c + 1)
                hi(gu2[0][:, c, :], w_gu[:, bass.ds(e * GU + c * 2 * F, 2 * F)], "gu_hi")

            def dn_hi(e, i, j, first=False):
                if not first:
                    act.wait_ge(s["edn"], len(FK) * (i - 1) + (1, 3)[j])
                hi(dn2[0][:, j, :], w_dn[:, bass.ds(e * DN + j * H, H)], "dn_hi")

            def silu(i):
                act.wait_ge(s["eg"], C * (i + 1))
                act.activation(silu_e[:, :], S[0][:, 0:F], ACT.Silu).then_inc(s["esil"], 1)

            def put_y(i, turn):
                act.wait_ge(s["edn"], len(FK) * (i + 1))
                act.wait_ge(s["dest_i"], i + 1)
                act.activation(y_sb[turn][:, :], A[:, :], ACT.Copy, scale=dest_i[turn][:, 1:2].bitcast(F32))\
                    .then_inc(s["ey"], 1)

            def aT_hi(i):
                act.wait_ge(s["Ta"], i + 1)
                hi(actT_e[0][:, :, :], S[3][:, 0:len(FK) * P].rearrange("p (k t) -> p k t", t=P), "aT_hi")

            def step(i, turn, first=False):
                e, e_next = experts(i)
                for c in range(C - 1):
                    gu_hi(e_next, i + 1, c)
                silu(i)
                xs_hi(i + 1)
                gu_hi(e_next, i + 1, C - 1)
                dn_hi(e, i, 0, first=first)
                if not first:
                    put_y(i - 1, 1 - turn)
                dn_hi(e, i, 1, first=first)
                aT_hi(i)

            act.wait_ge(s["pos"], 4)
            act.wait_ge(s["we"], 16 * (3 * E - 2 * n_late))
            xs_hi(0)
            for c in range(C):
                gu_hi(expert(0), 0, c, first=True)
            act.wait_ge(s["sdn"], NB * NJ)
            act.wait_ge(s["we_late"], 16 * 2 * n_late)
            step(0, 0, first=True)
            step(1, 1)
            assert NT % 2 == 1
            with act.Fori(2, NT - 2, 2) as i:
                step(i, 0)
                step(i + 1, 1)
            silu(NT - 1)
            e = expert(NT - 1)
            dn_hi(e, NT - 1, 0)
            act.wait_ge(s["edn"], len(FK) * (NT - 2) + 2)
            w = FK[-1][1]
            hi(dn2[0][0:w, 2, :], w_dn[0:w, bass.ds(e * DN + 2 * H, H)], "dn_hi")
            aT_hi(NT - 1)
            put_y(NT - 2, 1)
            dn_hi(e, NT - 1, 1)
            put_y(NT - 1, 0)

        @block.vector
        def _(dve):
            def stats(n, bn, mv, own_sem, done):
                dve.bn_stats(bn[:, n, :], xres[:, n, :]).then_inc(s[own_sem], 1)
                dve.wait_ge(s[own_sem], n + 1)
                dve.bn_aggr(mv[:, n, :], bn[:, n, :]).then_inc(s[done], 1)

            def apply(n, dst, mv, rs, ready, done):
                dve.wait_ge(s[ready], n + 1)
                dve.tensor_scalar(dst, xres[:, n, :], mv[:, n, 0:1], rs[:, n, :],
                                  ALU.subtract, ALU.mult).then_inc(s[done], 1)

            def lo(parts, src, hi_sem, value, sem, at):
                dve.wait_ge(s[hi_sem], value)
                hi_, lo_ = (t[at] for t in parts)
                dve.tensor_tensor(lo_, src, hi_.bitcast(F32), ALU.subtract).then_inc(s[sem], 1)

            def as_chunks(b, w=SQ):
                return b[:, 0:C * w].rearrange("p (c q) -> p c q", c=C)

            def stats1(n):
                stats(n, bn1, mv1, "bs1", "st1")

            def apply1(n):
                if n >= 2:
                    dve.wait_ge(s["T1"], n - 1)
                apply(n, xn[n % 2][:, :], mv1, rstd1, "rs1b", "xn")

            def xnT_lo(n, bank_):
                at = n % BLK * SQ
                lo(xnT[n // BLK], as_chunks(bank_), "xnT_hi", n + 1, "xnT_lo", (slice(None), slice(None), slice(at, at + SQ)))

            def add_attention(n):
                dve.wait_ge(s["op"], n + 1)
                dve.tensor_tensor(xres[:, n, :], xres[:, n, :], D[0:SQ, :], ALU.add).then_inc(s["x1"], 1)
                dve.wait_ge(s["x1"], n + 1)
                stats(n, bn2, mv2, "bs2", "st2")

            def apply2(n):
                apply(n, x2n[:, n, :], mv2, rstd2, "rs2b", "x2n")

            def x2T_lo(n):
                lo(x2T, as_chunks(B), "x2T_hi", n + 1, "x2T_lo", (slice(None), slice(None), slice(n * SQ, (n + 1) * SQ)))

            def sg_lo(j):
                at = (slice(None), slice(None), slice(0, 2 * FSK[j][1]))
                lo(w_sg2[j % 2], w_sg[j % 2][at], "wsg_hi", j + 1, "wsg_lo", at)

            def sd_lo(j):
                at = (slice(0, FSK[j][1]), slice(None))
                lo(w_sd2[j % 2], w_sd[j % 2][at], "wsd_hi", j + 1, "wsd_lo", at)

            def masked(b, r):
                dve.wait_ge(s["S"], R * b + r + 1)
                dve.scalar_tensor_tensor(out=score[r][:, :, :].rearrange("p c k -> p (c k)"),
                                         in0=S[r][0:SQ, 0:C * SQ], scalar=SCALE,
                                         in1=mask[:, :, :].rearrange("p c k -> p (c k)"),
                                         op0=ALU.mult, op1=ALU.add).then_inc(s["ms"], 1)
                dve.wait_ge(s["ms"], R * b + r + 1)
                dve.tensor_reduce(negmax[:, r, :], score[r][:, :, :], AX.X, ALU.max, negate=True)\
                   .then_inc(s["mask"], 1)

            def normalised(b, r):
                dve.wait_ge(s["exp"], R * b + r + 1)
                dve.reciprocal(rrow[:, r, :], rowsum[:, r, :]).then_inc(s["rr"], 1)
                if r == R - 1:
                    return
                dve.wait_ge(s["rr"], R * b + r + 1)
                dve.tensor_tensor(prob[r][:, :, :], prob[r][:, :, :],
                                  rrow[:, r, :].unsqueeze(2).to_broadcast([SQ, C, SQ]), ALU.mult)\
                   .then_inc(s["prob"], 1)

            whole = slice(None)
            dve.wait_ge(s["x0"], 16)
            stats1(0)

            def ctx_lo(k):
                dve.wait_ge(s[f"ctx{k}"], 16)
                at = slice(k * BLK, (k + 1) * BLK)
                lo(ctx2, ctx[:, at, :], "ctx_hi", k + 1, "ctx_lo", (whole, at, whole))

            ctx_lo(0)
            apply1(0)
            dve.wait_ge(s["wkv"], 16)
            keys = slice(0, H)
            lo(w_kv2, w_kv[:, keys], "wkv_hi", 1, "wkv_lo", (whole, keys))
            dve.wait_ge(s["x0b"], 16)
            stats1(1)
            stats1(2)
            apply1(1)
            xnT_lo(0, S[0])
            stats1(3)
            apply1(2)
            xnT_lo(1, S[1])
            apply1(3)
            dve.wait_ge(s["wq"], 16)
            half = slice(0, C // 2)
            lo(w_q2, w_q[:, half, :], "wq_hi", 2, "wq_lo", (whole, half, whole))
            for n in range(2, BLK):
                xnT_lo(n, S[n])
            ctx_lo(1)
            dve.wait_ge(s["xrest"], 16)
            stats1(BLK)
            for n in range(BLK, NB):
                if n + 1 < NB:
                    stats1(n + 1)
                apply1(n)
                if n > BLK:
                    xnT_lo(n - 1, S[n - 1 - BLK])
            xnT_lo(NB - 1, S[BLK - 1])
            dve.wait_ge(s["const"], 3)
            for r in range(R):
                masked(0, r)
            for r in range(R):
                normalised(0, r)
            for b in range(NB):
                for r in range(R):
                    if b + 1 < NB:
                        masked(b + 1, r)
                    if b >= 3 and r == 0 or b == 2 and r == 1:
                        x2T_lo(b - 2)
                if b == 2:
                    lo(w_gate2, w_gate[:, :, :], "wg_hi", 1, "wg_lo", (whole, whole, whole))
                if b >= 1:
                    add_attention(b - 1)
                if b + 1 < NB:
                    normalised(b + 1, 0)
                    normalised(b + 1, 1)
                if b >= 1:
                    apply2(b - 1)
                lo(oT, as_chunks(CC), "oT_hi", b + 1, "oT_lo", (whole, whole, whole))
                if b + 1 < NB:
                    normalised(b + 1, 2)
                    normalised(b + 1, 3)
                if b == 0:
                    sg_lo(0)
                    sd_lo(0)
                if b == NB - 1:
                    sg_lo(1)
                    sd_lo(1)
            add_attention(NB - 1)
            x2T_lo(NB - 2)
            apply2(NB - 1)

            def shared_act(j, t):
                k, w = FSK[j]
                n = NBLK * j + t
                dve.wait_ge(s["ssil"], n + 1)
                if j >= 1:
                    dve.wait_ge(s["sdn"], NB * (j - 1) + BLK * (t + 1))
                up = S[2 * t + 1][0:w, 0:W] if 2 * w > P else S[2 * t][w:2 * w, 0:W]
                dve.tensor_tensor(act_s[t][0:w, :], up, silu_s[t][0:w, :], ALU.mult).then_inc(s["sact"], 1)
                lo(act_s2[t], act_s[t][0:w, :], "sact_hi", n + 1, "sact_lo", (slice(0, w), whole))

            def add_shared(j, t, banks=range(BLK)):
                for i in banks:
                    b = t * BLK + i
                    dve.wait_ge(s["sdn"], NB * j + b + 1)
                    dve.tensor_tensor(xres[:, b, :], xres[:, b, :], (B, CC, D, A)[i][0:SQ, :], ALU.add)\
                       .then_inc(s["sres"], 1)

            cnt = [0]

            def link(ins):
                cnt[0] += 1
                ins.then_inc(s["rtc"], 1)
                dve.wait_ge(s["rtc"], cnt[0])

            def over_e(v):
                return v.unsqueeze(2).to_broadcast([SQ, NB, E])

            def pick(p, top, first, oh):
                link(dve.tensor_reduce(top, p[:, :, :], AX.X, ALU.max))
                link(dve.tensor_tensor(eq[:, :, :], p[:, :, :], over_e(top), ALU.is_equal))
                link(dve.tensor_tensor(cand[:, :, :], eq[:, :, :], down8[:, :, :], ALU.mult))
                link(dve.tensor_reduce(first[:, :], cand[:, :, :], AX.X, ALU.max))
                link(dve.tensor_tensor(oh[:, :, :], down8[:, :, :], over_e(first[:, :]), ALU.is_equal))

            shared_act(0, 0)
            x2T_lo(NB - 1)
            shared_act(0, 1)
            sg_lo(2)
            dve.wait_ge(s["lg"], 1)
            dve.wait_ge(s["const"], 4)
            lg = A[0:SQ, 0:NB * E].rearrange("p (b e) -> p b e", e=E)
            link(dve.tensor_reduce(lmax[:, :], lg, AX.X, ALU.max))
            dve.tensor_tensor(logit[:, :, :], lg, over_e(lmax[:, :]), ALU.subtract).then_inc(s["rt"], 1)
            dve.wait_ge(s["lexp"], 1)
            link(dve.tensor_reduce(lsum[:, :], pexp[:, :, :], AX.X, ALU.add))
            link(dve.reciprocal(lrec[:, :], lsum[:, :]))
            link(dve.tensor_tensor(prb[:, :, :], pexp[:, :, :], over_e(lrec[:, :]), ALU.mult))
            pick(prb, topw[:, 0, :], first1, oh1)
            link(dve.scalar_tensor_tensor(out=prb2[:, :, :], in0=oh1[:, :, :], scalar=-2.0, in1=prb[:, :, :],
                                          op0=ALU.mult, op1=ALU.add))
            pick(prb2, topw[:, 1, :], first2, oh2)
            link(dve.tensor_tensor(picked[:, 0:NB, :], oh1[:, :, :], oh2[:, :, :], ALU.add))
            for b in range(NB):
                last = dve.tensor_tensor(before[:, b + 1, :], before[:, b, :], picked[:, b, :], ALU.add)
                if b < NB - 1:
                    link(last)
            last.then_inc(s["trip"], 1)
            add_shared(0, 0)
            shared_act(1, 0)
            add_shared(0, 1)
            shared_act(1, 1)
            sg_lo(3)
            sd_lo(2)
            dve.wait_ge(s["rank"], 2)
            dve.tensor_copy(rank[:, :, :], A[0:SQ, 0:NB * E].rearrange("p (b e) -> p b e", e=E)).then_inc(s["rk"], 1)
            dve.tensor_copy(count[:, :], A[:, NB * E:(NB + 1) * E]).then_inc(s["rk"], 1)
            dve.wait_ge(s["rk"], 2)
            link(dve.tensor_tensor(overs[:, :, :], count[:, :].unsqueeze(2).to_broadcast([P, E, T // P]),
                                   thresh[:, :, :], ALU.is_gt))
            link(dve.tensor_reduce(tiles[:, :], overs[:, :, :], AX.X, ALU.add))
            link(dve.tensor_tensor(tilesb[:, :, :], tiles[:, :].unsqueeze(1).to_broadcast([P, E, E]),
                                   below[:, :, :], ALU.mult))
            link(dve.tensor_reduce(base[:, :], tilesb[:, :, :], AX.X, ALU.add))
            link(dve.scalar_tensor_tensor(out=slot[:, :, :], in0=base[0:SQ, :].unsqueeze(1).to_broadcast([SQ, NB, E]),
                                          scalar=float(P), in1=rank[:, :, :],
                                          op0=ALU.mult, op1=ALU.add))
            link(dve.tensor_tensor(slot1[:, :, :], slot[:, :, :], oh1[:, :, :], ALU.mult))
            link(dve.tensor_tensor(slot2[:, :, :], slot[:, :, :], oh2[:, :, :], ALU.mult))
            with nc.allow_low_precision(reason="slots are whole numbers under 2^24, exact in both types"):
                dve.tensor_reduce(slot_i[:, 0, :], slot1[:, :, :], AX.X, ALU.add).then_inc(s["pos"], 1)
                dve.tensor_reduce(slot_i[:, 1, :], slot2[:, :, :], AX.X, ALU.add).then_inc(s["pos"], 1)
            link(dve.tensor_tensor(started[:, :, :], tile_no[:, :, :], base[0:1, :].unsqueeze(1).to_broadcast([1, NT, E]),
                                   ALU.is_ge))
            link(dve.tensor_reduce(eid_f[:, :], started[:, :, :], AX.X, ALU.add))
            link(dve.scalar_tensor_tensor(out=pair_f[:, :], in0=eid_f[:, 1:NT], scalar=float(E), in1=eid_f[:, 0:NT - 1],
                                          op0=ALU.mult, op1=ALU.add))
            dve.tensor_scalar(eid2[:, :], pair_f[:, :], -1.0 - E, None, ALU.add).then_inc(s["pos"], 1)
            dve.tensor_scalar(eid[:, :], eid_f[:, :], -1.0, None, ALU.add).then_inc(s["pos"], 1)
            for j in range(2, NJ):
                for t in range(NBLK):
                    add_shared(j - 1, t)
                    shared_act(j, t)
                if j + 2 < NJ:
                    sg_lo(j + 2)
                if j + 1 < NJ:
                    sd_lo(j + 1)
            add_shared(NJ - 1, 0)

            def xs_lo(i):
                lo(xsT, as_chunks(S[2], P), "xs_hi", i + 1, "xs_lo", (whole, whole, whole))

            def expert(i):
                return dve.value_load(eid[0:1, bass.ds(i, 1)], min_val=0, max_val=E - 1)

            def experts(i):
                both_ = dve.value_load(eid2[0:1, bass.ds(i, 1)], min_val=0, max_val=E * E - 1)
                return both_ % E, both_ // E

            def gu_lo(e, i, c):
                lo(gu2, w_gu[:, bass.ds(e * GU + c * 2 * F, 2 * F)], "gu_hi", C * i + c + 1, "gu_lo", (whole, c, whole))

            def dn_lo(e, i):
                lo(dn2, w_dn[:, bass.ds(e * DN, H)], "dn_hi", 2 * i + 1, "dn_lo", (whole, 0, whole))

            def expert_act(i):
                dve.wait_ge(s["esil"], i + 1)
                dve.tensor_tensor(act_e[:, 0:F], S[1][:, 0:F], silu_e[:, :], ALU.mult).then_inc(s["eact"], 1)

            def aT_lo(i):
                lo(actT_e, S[3][:, 0:len(FK) * P].rearrange("p (k t) -> p k t", t=P), "aT_hi", i + 1, "aT_lo",
                   (whole, whole, whole))

            def step_e(i):
                e, e_next = experts(i)
                for c in range(2):
                    gu_lo(e_next, i + 1, c)
                expert_act(i)
                xs_lo(i + 1)
                for c in range(2, C):
                    gu_lo(e_next, i + 1, c)
                dn_lo(e, i)
                aT_lo(i)

            dve.memset(act_e[:, F:len(FK) * P], 0.0).then_inc(s["pad_act"], 1)
            xs_lo(0)
            for c in range(C - 1):
                gu_lo(expert(0), 0, c)
            add_shared(NJ - 1, 1, [BLK - 1])
            gu_lo(expert(0), 0, C - 1)
            step_e(0)
            add_shared(NJ - 1, 1, range(BLK - 1))
            with dve.Fori(1, NT - 1) as i:
                step_e(i)
            expert_act(NT - 1)
            e = expert(NT - 1)
            dn_lo(e, NT - 1)
            for n, j in ((2, 2), (3, 1)):
                w = FK[j][1]
                lo(dn2, w_dn[0:w, bass.ds(e * DN + j * H, H)], "dn_hi", 2 * (NT - 1) + n, "dn_lo_end",
                   (slice(0, w), j, whole))
                if j == 2:
                    aT_lo(NT - 1)


def kernel(x, ctx_512, L0_xattn_Wq, L0_xattn_Wkv_expand, L0_xattn_Wout, L0_ffn_gate_weight,
           L0_ffn_gate_up_weights, L0_ffn_down_weights, L0_ffn_shared_gate_up, L0_ffn_shared_down):
    import concourse.bacc as bacc
    from concourse.bass_utils import run_bass_kernel_spmd

    def by_rows(w):
        t = np.swapaxes(np.asarray(w), -1, -2)
        t = t.reshape(*t.shape[:-2], t.shape[-2] // P, P, t.shape[-1])
        return np.swapaxes(t, -3, -2)

    arrays = {
        "x": x,
        "ctxT": np.asarray(ctx_512).transpose(2, 0, 1),
        "wqT": np.asarray(L0_xattn_Wq).T,
        "wkvT": np.asarray(L0_xattn_Wkv_expand).T,
        "woT": np.asarray(L0_xattn_Wout).T,
        "gateT": by_rows(L0_ffn_gate_weight),
        "guT": by_rows(L0_ffn_gate_up_weights),
        "dnT": np.swapaxes(np.asarray(L0_ffn_down_weights), 1, 2),
        "sguT": by_rows(L0_ffn_shared_gate_up),
        "sdnT": np.asarray(L0_ffn_shared_down).T,
    }
    arrays = {n: np.ascontiguousarray(a) for n, a in arrays.items()}
    nc = bacc.Bacc("TRN2", target_bir_lowering=False, num_devices=1, dynamic_dma_scratch_size=8192)
    args = [nc.dram_tensor(n, a.shape, F32, kind="ExternalInput").ap() for n, a in arrays.items()]
    out = nc.dram_tensor("out", x.shape, F32, kind="ExternalOutput").ap()
    build(nc, *args, out)
    result = run_bass_kernel_spmd(nc, [arrays], core_ids=[0])
    return result.results[0]["out"]
```
